# Optimizing a Trainium2 kernel written in Bass

```python
import numpy as np
import jax
import jax.numpy as jnp

def _softmax(x, axis=-1):
    return jax.nn.softmax(x, axis=axis)

def _gelu(x):
    return jax.nn.gelu(x, approximate=True)

def _silu(x):
    return jax.nn.silu(x)

def _sigmoid(x):
    return jax.nn.sigmoid(x)

def _layernorm(x, axis=-1, eps=1e-05):
    m = jnp.mean(x, axis=axis, keepdims=True)
    v = jnp.var(x, axis=axis, keepdims=True)
    return (x - m) / jnp.sqrt(v + eps)

def _scatter_add(tgt, idx, src, axis=0):
    return tgt.at[idx].add(src)

def _segment_sum(src, seg, n):
    return jax.ops.segment_sum(src, seg, n)
kernel_name = 'mk_gnn_resnorm_d1_gnn_r32_ce6c53'

def setup_inputs(seed: int=0):
    np.random.seed(seed)
    _w = jnp.asarray

    def _rec_inputs():
        import jax
        import jax.numpy as jnp
        _gk = jax.random.key(seed)
        x = -0.000202 + 1 * jax.random.normal(jax.random.fold_in(_gk, 1), (3125, 128), jnp.float32)
        _s = jax.random.randint(jax.random.fold_in(_gk, 2), (25000,), 0, 3125, jnp.int32)
        _d = jax.random.randint(jax.random.fold_in(_gk, 3), (25000,), 0, 3125, jnp.int32)
        _loop = jnp.arange(3125, dtype=jnp.int32)
        src = jnp.concatenate([_s, _d, _loop])
        dst = jnp.concatenate([_d, _s, _loop])
        _o = jnp.argsort(dst, stable=True)
        src = src[_o]
        dst = dst[_o]
        edge_attr_64 = -5.16925e-05 + 1.00005 * jax.random.normal(jax.random.fold_in(_gk, 12), (53125, 64), jnp.float32)
        return (x, src, dst, edge_attr_64)
    x, src, dst, edge_attr_64 = _rec_inputs()

    def _L0_gnn_setup():
        import jax, jax.numpy as jnp
        import numpy as np
        N_NODES = 50000
        N_EDGES = 50000
        F_NODE = 128
        F_EDGE = 64
        L = 128
        EPS = 1e-05

        def _bn(h, gamma, beta):
            mu = jnp.mean(h, axis=0, keepdims=True)
            var = jnp.mean((h - mu) ** 2, axis=0, keepdims=True)
            return (h - mu) * jax.lax.rsqrt(var + EPS) * gamma + beta
        key = jax.random.key(seed)
        ks = jax.random.split(key, 12)
        e1 = F_NODE + F_EDGE
        e2 = F_NODE + L
        inp = {'x': jax.random.normal(ks[0], (N_NODES, F_NODE), jnp.float32), 'edge_index': jax.random.randint(ks[1], (2, N_EDGES), 0, N_NODES, jnp.int32), 'edge_attr': jax.random.normal(ks[2], (N_EDGES, F_EDGE), jnp.float32), 'u': jax.random.normal(ks[3], (1, 4), jnp.float32), 'batch': jnp.zeros((N_NODES,), jnp.int32), 'W1': jax.random.normal(ks[4], (e1, L), jnp.float32) / np.sqrt(e1), 'b1': jnp.zeros((L,), jnp.float32), 'g1': jnp.ones((L,), jnp.float32), 'be1': jnp.zeros((L,), jnp.float32), 'W2': jax.random.normal(ks[5], (e2, e2), jnp.float32) / np.sqrt(e2), 'b2': jnp.zeros((e2,), jnp.float32), 'g2': jnp.ones((e2,), jnp.float32), 'be2': jnp.zeros((e2,), jnp.float32), 'Wl': jax.random.normal(ks[6], (e2, F_NODE), jnp.float32) / np.sqrt(e2), 'bl': jnp.zeros((F_NODE,), jnp.float32)}
        return inp
    _L0_gnn_all = _L0_gnn_setup()
    _L0_gnn_in = {k: v for k, v in _L0_gnn_all.items() if k in ('u', 'W1', 'b1', 'g1', 'be1', 'W2', 'b2', 'g2', 'be2', 'Wl', 'bl')}
    del _L0_gnn_all
    return {'x': x, 'src': src, 'dst': dst, 'edge_attr_64': edge_attr_64, 'L0_gnn_u': _L0_gnn_in['u'], 'L0_gnn_W1': _L0_gnn_in['W1'], 'L0_gnn_b1': _L0_gnn_in['b1'], 'L0_gnn_g1': _L0_gnn_in['g1'], 'L0_gnn_be1': _L0_gnn_in['be1'], 'L0_gnn_W2': _L0_gnn_in['W2'], 'L0_gnn_b2': _L0_gnn_in['b2'], 'L0_gnn_g2': _L0_gnn_in['g2'], 'L0_gnn_be2': _L0_gnn_in['be2'], 'L0_gnn_Wl': _L0_gnn_in['Wl'], 'L0_gnn_bl': _L0_gnn_in['bl']}

def reference(x, src, dst, edge_attr_64, L0_gnn_u, L0_gnn_W1, L0_gnn_b1, L0_gnn_g1, L0_gnn_be1, L0_gnn_W2, L0_gnn_b2, L0_gnn_g2, L0_gnn_be2, L0_gnn_Wl, L0_gnn_bl):
    import jax
    import jax.numpy as jnp

    def _L0_gnn_ref(x, edge_index, edge_attr, u, batch, W1, b1, g1, be1, W2, b2, g2, be2, Wl, bl):
        import jax, jax.numpy as jnp
        import numpy as np
        N_NODES = 50000
        N_EDGES = 50000
        F_NODE = 128
        F_EDGE = 64
        L = 128
        EPS = 1e-05

        def _bn(h, gamma, beta):
            mu = jnp.mean(h, axis=0, keepdims=True)
            var = jnp.mean((h - mu) ** 2, axis=0, keepdims=True)
            return (h - mu) * jax.lax.rsqrt(var + EPS) * gamma + beta
        n = x.shape[0]
        row, col = (edge_index[0], edge_index[1])
        h = jnp.concatenate([x[row], edge_attr], axis=1)
        h = jax.nn.relu(_bn(h @ W1 + b1, g1, be1))
        s = jax.ops.segment_sum(h, col, num_segments=n)
        cnt = jax.ops.segment_sum(jnp.ones((h.shape[0], 1), h.dtype), col, num_segments=n)
        agg = jnp.where(cnt > 0, s / jnp.maximum(cnt, 1.0), 0.0)
        h2 = jnp.concatenate([x, agg], axis=1)
        h2 = jax.nn.relu(_bn(h2 @ W2 + b2, g2, be2))
        return jax.nn.relu(h2 @ Wl + bl)
    edge_index = jnp.stack([src, dst])
    batch0 = jnp.zeros((3125,), jnp.int32)
    x = _layernorm(x + _L0_gnn_ref(x, edge_index, edge_attr_64, L0_gnn_u, batch0, L0_gnn_W1, L0_gnn_b1, L0_gnn_g1, L0_gnn_be1, L0_gnn_W2, L0_gnn_b2, L0_gnn_g2, L0_gnn_be2, L0_gnn_Wl, L0_gnn_bl), axis=-1)
    return x

_drawn_inputs = setup_inputs


def setup_inputs(seed=0):
    import zlib

    import numpy as np

    out = dict(_drawn_inputs(seed))
    spreads = {'L0_gnn_b1': (0.0, 0.8),
     'L0_gnn_g1': (1.0, 0.6),
     'L0_gnn_be1': (0.0, 0.8),
     'L0_gnn_b2': (0.0, 0.8),
     'L0_gnn_g2': (1.0, 0.2),
     'L0_gnn_be2': (0.0, 0.1),
     'L0_gnn_bl': (0.0, 0.1)}
    factors = {}
    for name, (base, spread) in spreads.items():
        noise = np.random.default_rng([zlib.crc32(name.encode()), seed]).standard_normal(out[name].shape)
        drawn = base * np.exp(spread * noise) if base else spread * noise
        out[name] = jnp.asarray(drawn.astype(out[name].dtype))
    for name, factor in factors.items():
        out[name] = (out[name] * factor).astype(out[name].dtype)
    return out
```

```python
from contextlib import ExitStack

import concourse.bass as bass
from concourse import mybir

F32 = mybir.dt.float32
BF16 = mybir.dt.bfloat16
I32 = mybir.dt.int32
ALU = mybir.AluOpType
ACT = mybir.ActivationFunctionType
AX_X = mybir.AxisListType.X

P = 128
EPS = 1e-5
TINY = 1e-20
TILES = 4
GROUP = TILES * P
U = 4
KEEP = 3
WIN = 64
WIDE = 512


def gnn_kernel(nc, x, src, dst, ea, W1, b1, g1, be1, W2, b2, g2, be2, Wl, bl, out):
    N, F = x.shape
    E, FE = ea.shape
    H2 = W2.shape[1] // P
    NT = 25
    PN = N // NT
    NG = (E + GROUP - 1) // GROUP
    NI = NG // U
    assert F == P and FE * 2 == P and NT * PN == N and NG == NI * U and H2 == 2
    LAST = E - (NG - 1) * GROUP
    LP = LAST // TILES
    LR = LAST - LP * TILES
    PAD = N
    YROWS = 25 * P
    NAGG = N + WIN
    CH = 4 * PN
    CHUNKS = [(c, min(CH, N - c)) for c in range(0, N, CH)]
    NC = len(CHUNKS)
    WBLOCKS = [(b, min(WIDE, N - b)) for b in range(0, N, WIDE)]

    ytab = nc.dram_tensor("ytab", (YROWS, F), F32, kind="Internal").ap()
    xt_dram = nc.dram_tensor("xt_dram", (P, N), F32, kind="Internal").ap()
    spill = nc.dram_tensor("spill", (NI, P, TILES * F), F32, kind="Internal").ap()

    ctx = ExitStack()
    with ctx:
        def sb(name, shape, dt=F32):
            return ctx.enter_context(nc.sbuf_tensor(name, shape, dt))

        def pb(name, shape):
            return ctx.enter_context(nc.psum_tensor(name, shape, F32))

        def sem(name):
            return ctx.enter_context(nc.semaphore(name))

        GF = TILES * F
        res = sb("res", [P, NI * KEEP * GF])
        work = sb("work", [P, 6, GF])
        yg = work[:, 0:2, :]
        hs = work[:, 2:4, :]
        sq = work[:, 4:6, :]
        mx = work[:, 0:4, :]
        back = work[:, 4, :]
        work2 = sb("work2", [P, 4, TILES * WIN])
        ear = work2[:, 0:2, :]
        eat = work2[:, 2:4, :]
        hotf = work2
        hotb = sb("hotb", [P, 2, TILES * WIN], BF16)
        agg = sb("agg", [P, NAGG])
        cnt = sb("cnt", [P, NAGG])
        srci = sb("srci", [P, TILES, NG], I32)
        idx = sb("idx", [P, U, TILES], I32)
        locr = sb("locr", [P, U, TILES])
        loc = sb("loc", [P, TILES, NG])
        basei = sb("basei", [1, NG], I32)
        ident = sb("ident", [P, P])
        w1x = sb("w1x", [P, F])
        w1e = sb("w1e", [P, 2, F])
        negu = sb("negu", [P, F])
        iota = sb("iota", [P, WIN])
        ones = sb("ones", [P, 1])
        onesb = sb("onesb", [P, P], BF16)
        zero2 = sb("zero2", [P, 2])
        col = sb("col", [P, 24])
        rowc = sb("rowc", [1, 4])
        rowi = sb("rowi", [1, 4], I32)

        at = NI * KEEP * GF

        def tail(n):
            nonlocal at
            at -= n
            return res[:, at:at + n]

        xn0 = tail(NT * F)
        ysb = tail(NT * F)
        xt0 = tail(N)
        srow = tail(GROUP)
        drow = tail(GROUP)
        srowf = tail(GROUP)
        drowf = tail(GROUP)
        rowst = tail(4)
        zeros = tail(F)
        sgn = tail(F)
        gbc = tail(F)

        near = 0

        def head(n):
            nonlocal near
            near += n
            return res[:, near - n:near]

        xt = head(N)
        xn = head(NT * F)
        w2 = head(2 * H2 * P)
        wl = head(H2 * F)
        blr = head(F)
        HEAD_STEPS = near // (KEEP * GF) + 2
        h2 = head(H2 * N)
        h2r = head(H2 * N)
        z = head(NT * F)
        zo = head(NT * F)
        bs2 = head(H2 * NC * 6)
        bs3 = head(NT * 6)
        mv3 = head(NT * 2)
        rs3 = head(NT)
        colh = head(16)
        mv2 = head(2 * H2)

        psT = [pb(f"psT{i}", [P, 2 * P]) for i in range(2)]
        psH = [pb(f"psH{i}", [P, GF]) for i in range(2)]
        psC = [pb(f"psC{i}", [P, GF]) for i in range(2)]
        psS = pb("psS", [P, 512])
        psX = pb("psX", [P, 512])
        psA = [psH[0], psH[1], psC[0], psC[1]]

        BANK = psA

        s_x = sem("x_loaded")
        s_w = sem("w_loaded")
        s_rowset = sem("rows_preset")
        s_rows = sem("rows_loaded")
        s_cols = sem("cols_loaded")
        s_ident = sem("ident_ready")
        s_pool = sem("pool_chain")
        s_wsgn = sem("w1_signed")
        s_dv = sem("dve_chain")
        s_rowf = sem("rows_as_float")
        s_rowt = sem("rows_turned")
        s_idx = sem("indices_ready")
        s_xps = sem("x_turned_psum")
        s_xt = sem("xt_ready")
        s_yps = sem("y_psum")
        s_ysb = sem("y_ready")
        s_zr = sem("zeros_ready")
        s_tab = sem("tables_written")
        ea_loaded = [sem(f"ea_loaded{i}") for i in range(2)]
        ea_turned = sem("ea_turned")
        eat_ready = sem("eat_ready")
        prod_ready = sem("ea_product_ready")
        idx_staged = sem("idx_staged")
        gathered = [sem(f"gathered{i}") for i in range(2)]
        h_ready = sem("h_ready")
        sq_ready = sem("sq_ready")
        stats_done = sem("stats_done")
        kept = sem("kept")
        spilled = sem("spilled")
        hotb_ready = sem("hotb_ready")
        cnt_ps = sem("cnt_psum_ready")
        cnt_added = sem("cnt_added")
        s_set = sem("memory_preset")
        s_bn1 = sem("bn1_chain")
        s_sqrt1 = sem("bn1_sqrt")
        s_uin = sem("diag_u_ready")
        s_ups = sem("u_spread")
        s_u = sem("negu_ready")
        reload = sem("group_back")
        slot_passed = sem("slot_passed")
        loc_staged = sem("loc_staged")
        hotf_ready = sem("hotf_ready")
        m_ready = sem("max_ready")
        summed = sem("window_summed")
        agg_added = sem("agg_added")
        s_nodein = sem("node_inputs_loaded")
        s_tail = sem("tail_chain")
        s_aggm = sem("mean_ready")
        s_h2ps = sem("h2_psum")
        s_h2 = sem("h2_copied")
        s_h2st = sem("h2_stats")
        s_bn2 = sem("bn2_chain")
        s_sqrt2 = sem("bn2_sqrt")
        s_h2r = sem("h2_relu")
        s_ops = sem("out_psum")
        s_z = sem("z_ready")
        s_zst = sem("z_stats")
        s_sqrt3 = sem("ln_sqrt")
        s_ln = sem("ln_scale_ready")
        s_zo = sem("out_rows_ready")
        s_out = sem("out_written")

        C_SUM, C_G, C_BE, C_B1, C_M, C_Q, C_V, C_SD, C_R, C_S, C_T, C_U, C_AG = range(13)

        def c(i, n=1):
            return col[:, i:i + n]

        def resg(i, q):
            return res[:, bass.ds((i * KEEP + q) * GF, GF)]

        def first(i, q, back_by):
            return isinstance(i, int) and U * i + q < back_by

        block = ctx.enter_context(nc.Block())

        @block.sync
        def _(sp):
            sp.dma_start(xn0[0:PN, :], x.rearrange("(p t) f -> p (t f)", t=NT)).then_inc(s_x, 16)
            sp.wait_ge(s_rowset, 1)
            for r, d in ((srow, src), (drow, dst)):
                sp.dma_start(r[0:NG - 1, :].bitcast(I32),
                             d[0:(NG - 1) * GROUP].rearrange("(g e) -> g e", e=GROUP)).then_inc(s_rows, 16)
                sp.dma_start(r[NG - 1:NG, 0:LAST].bitcast(I32),
                             d[(NG - 1) * GROUP:E].rearrange("(g e) -> g e", g=1)).then_inc(s_rows, 16)
            sp.wait_ge(s_xt, NT)
            sp.dma_start(xt_dram, xt0[:, :]).then_inc(s_tab, 16)
            sp.wait_ge(s_zr, 1)
            sp.dma_start(ytab[N:YROWS, :], zeros[0:YROWS - N, :]).then_inc(s_tab, 16)
            sp.wait_ge(s_ysb, NT)
            sp.dma_start(ytab[0:N, :].rearrange("(p t) f -> p (t f)", t=NT), ysb[0:PN, :]).then_inc(s_tab, 16)

            def load_ea(i, q):
                if not first(i, q, 2):
                    sp.wait_ge(ea_turned, U * i + q - 1)
                s = ea_loaded[q % 2]
                sp.dma_start(ear[:, q % 2, :],
                             ea[bass.ds((i * U + q) * GROUP, GROUP), :].rearrange(
                                 "(p j) f -> p (j f)", j=TILES)).then_inc(s, 16)

            for q in range(U):
                load_ea(0, q)
            with sp.Fori(1, NI - 1) as i:
                for q in range(U):
                    load_ea(i, q)
            for q in range(U - 1):
                load_ea(NI - 1, q)
            sp.wait_ge(ea_turned, NG - 2)
            sp.wait_ge(s_tab, 48)
            e0 = (NG - 1) * GROUP
            s = ea_loaded[1]
            sp.dma_start(ear[0:LP, 1, :],
                         ea[e0:e0 + LP * TILES, :].rearrange("(p j) f -> p (j f)", j=TILES)).then_inc(s, 16)
            sp.dma_start(ear[LP:LP + 1, 1, 0:LR * FE],
                         ea[e0 + LP * TILES:E, :].rearrange("(p j) f -> p (j f)", p=1)).then_inc(s, 16)
            zr = ytab[N:YROWS, :].rearrange("r f -> (r f)")
            n1 = (TILES - LR) * FE
            sp.dma_start(ear[LP:LP + 1, 1, LR * FE:],
                         zr[0:n1].rearrange("(p f) -> p f", p=1)).then_inc(s, 16)
            n2 = (P - LP - 1) * TILES * FE
            sp.dma_start(ear[LP + 1:P, 1, :],
                         zr[n1:n1 + n2].rearrange("(p f) -> p f", f=TILES * FE)).then_inc(s, 16)

            sp.wait_ge(spilled, 16 * NI)
            sp.wait_ge(stats_done, NG)
            sp.dma_start(back, spill[0, :, :]).then_inc(reload, 16)
            sp.wait_ge(m_ready, 1)
            sp.wait_ge(reload, 16)
            sp.dma_start(resg(0, 0), spill[1, :, :]).then_inc(reload, 16)
            with sp.Fori(1, NI - 1) as i:
                sp.wait_ge(m_ready, U * i + 1)
                sp.wait_ge(reload, 16 * (i + 1))
                sp.dma_start(resg(i, 0), spill[bass.ds(i + 1, 1), :, :].rearrange("a p f -> (a p) f")
                             ).then_inc(reload, 16)
            sp.dma_start(xt, xt_dram).then_inc(s_nodein, 16)
            sp.dma_start(xn[0:PN, :], x.rearrange("(p t) f -> p (t f)", t=NT)).then_inc(s_nodein, 16)
            sp.dma_start(w2.rearrange("p (k c) -> p k c", k=2), W2.rearrange("(k p) c -> p k c", k=2)
                         ).then_inc(s_nodein, 16)
            sp.dma_start(wl.rearrange("p (k c) -> p k c", k=H2), Wl.rearrange("(k p) c -> p k c", k=H2)
                         ).then_inc(s_nodein, 16)
            sp.dma_start(blr[0:PN, :], bl.partition_broadcast(PN)).then_inc(s_nodein, 16)
            for k, v in enumerate((g2, be2, b2)):
                for h in range(H2):
                    sp.dma_start(colh[:, 2 * k + h:2 * k + h + 1],
                                 v[h * P:(h + 1) * P].rearrange("(p a) -> p a", a=1)).then_inc(s_nodein, 16)
            for k in range(5):
                t0, t1 = 5 * k, 5 * k + 5
                sp.wait_ge(s_zo, 5 * k + 5)
                sp.dma_start(out.rearrange("(p t) f -> p t f", t=NT)[:, t0:t1, :],
                             zo[0:PN, :].rearrange("p (t f) -> p t f", t=NT)[:, t0:t1, :]).then_inc(s_out, 16)
            sp.wait_ge(s_out, 16 * 5)

        @block.gpsimd
        def _(pool):
            pool.memset(srow.bitcast(I32), PAD)
            pool.memset(drow.bitcast(I32), PAD).then_inc(s_rowset, 1)
            pool.memset(ident[:, :], 0.0).then_inc(s_pool, 1)
            pool.wait_ge(s_pool, 1)
            pool.affine_select(out=ident[:, :], in_=ident[:, :], compare_op=ALU.not_equal, fill=1.0, base=0,
                               pattern=[[-1, P]], channel_multiplier=1).then_inc(s_ident, 1)
            pool.memset(zeros, 0.0).then_inc(s_zr, 1)
            pool.iota(iota[:, :], [[1, WIN]], base=0, channel_multiplier=0,
                      allow_small_or_imprecise_dtypes=True)
            pool.memset(onesb[:, :], 1.0)
            pool.memset(ones[:, :], 1.0)
            pool.memset(zero2[:, :], 0.0)
            pool.memset(cnt[:, :], 0.0)
            pool.memset(agg[:, :], 0.0).then_inc(s_set, 1)
            pool.wait_ge(s_idx, 1)
            pool.wait_ge(s_tab, 48)

            def gather(i, q):
                if not first(i, q, 2):
                    pool.wait_ge(h_ready, U * i + q - 1)
                pool.wait_ge(idx_staged, U * i + q + 1)
                pool.sem_inc(slot_passed, 1)
                for j in range(TILES):
                    pool.indirect_dma_start(
                        yg[:, q % 2, j * F:(j + 1) * F], None, ytab,
                        bass.IndirectOffsetOnAxis(ap=idx[:, q, j:j + 1], axis=0)
                    ).then_inc(gathered[q % 2], 16)

            for q in range(U):
                gather(0, q)
            with pool.Fori(1, NI) as i:
                for q in range(U):
                    gather(i, q)

            def onehot_f(i, q):
                if not first(i, q, 4):
                    pool.wait_ge(summed, U * i + q - 3)
                pool.wait_ge(loc_staged, U * i + q + 1)
                pool.sem_inc(slot_passed, 1)
                for j in range(TILES):
                    last = pool.tensor_scalar(hotf[:, q, j * WIN:(j + 1) * WIN], iota[:, :],
                                              locr[:, q, j:j + 1], None, ALU.is_equal)
                last.then_inc(hotf_ready, 1)

            pool.wait_ge(ea_turned, NG)
            pool.wait_ge(prod_ready, NG)
            for q in range(U):
                onehot_f(0, q)
            with pool.Fori(1, NI) as i:
                for q in range(U):
                    onehot_f(i, q)

        @block.tensor
        def _(pe):
            pe.wait_ge(s_ident, 1)
            pe.wait_ge(s_x, 16)
            xv = xn0[0:PN, :].rearrange("p (t f) -> p t f", t=NT)
            xtv = xt0.rearrange("f (p t) -> f t p", t=NT)

            def turn_x(t):
                if t >= 2:
                    pe.wait_ge(s_xt, t - 1)
                pe.transpose(psC[t % 2][:, 0:PN], xv[:, t, :], ident[0:PN, 0:PN]).then_inc(s_xps, 1)

            def y_tile(t):
                pe.wait_ge(s_xt, t + 1)
                if t == 0:
                    pe.wait_ge(s_wsgn, 2)
                if t >= 2:
                    pe.wait_ge(s_ysb, t - 1)
                pe.matmul(psH[t % 2][0:PN, 0:F], xtv[:, t, :], w1x[:, :], start=True, stop=True).then_inc(s_yps, 1)

            turn_x(0)
            for t in range(NT):
                if t + 1 < NT:
                    turn_x(t + 1)
                y_tile(t)
            pe.wait_ge(s_rowf, 2)
            for k, r in enumerate((srowf, drowf)):
                rv = r[0:NG, :].rearrange("g (p j) -> g j p", j=TILES)
                for j in range(TILES):
                    last = pe.transpose((psS, psX)[k][:, j * NG:(j + 1) * NG], rv[:, j, :], ident[0:NG, 0:NG])
                last.then_inc(s_rowt, 1)
            pe.transpose(psT[0][0:1, 0:NG], rowst[0:NG, 0:1], ident[0:NG, 0:NG])
            pe.transpose(psT[1][0:1, 0:NG], rowst[0:NG, 2:3], ident[0:NG, 0:NG]).then_inc(s_rowt, 1)
            pe.wait_ge(s_idx, 1)
            pe.wait_ge(s_set, 1)
            pe.matmul(psS[:, 0:2], ident[:, :], zero2[:, :], start=True, stop=False, skip_group_check=True)

            def product(i, q):
                g = U * i + q
                pe.wait_ge(ea_loaded[q % 2], 16 * (2 * i + q // 2 + 1) if not (isinstance(i, int) and g == NG - 1)
                           else 16 * (2 * i + q // 2 + 4))
                if not first(i, q, 2):
                    pe.wait_ge(eat_ready, g - 1)
                for b in range(2):
                    last = pe.transpose(psT[q % 2][:, b * P:(b + 1) * P], ear[:, q % 2, b * P:(b + 1) * P], ident[:, :])
                last.then_inc(ea_turned, 1)
                pe.wait_ge(eat_ready, g + 1)
                if not first(i, q, 2):
                    pe.wait_ge(h_ready, g - 1)
                for b in range(2):
                    last = pe.matmul(psH[q % 2][:, b * 2 * F:(b + 1) * 2 * F], eat[:, q % 2, b * P:(b + 1) * P],
                                     w1e[:, :, :].rearrange("p a f -> p (a f)"), start=True, stop=True)
                last.then_inc(prod_ready, 1)

            def counts(i, q):
                g = U * i + q
                pe.wait_ge(hotb_ready, g + 1)
                if not first(i, q, 2):
                    pe.wait_ge(cnt_added, g - 1)
                for j in range(TILES):
                    last = pe.matmul(psC[q % 2][:, 0:WIN], onesb[:, :], hotb[:, q % 2, j * WIN:(j + 1) * WIN],
                                     start=(j == 0), stop=(j == TILES - 1))
                last.then_inc(cnt_ps, 1)

            def stats(i, q):
                g = U * i + q
                pe.wait_ge(h_ready, g + 1)
                for j in range(TILES):
                    pe.matmul(psS[:, 0:1], hs[:, q % 2, j * F:(j + 1) * F], ones[:, :], start=False, stop=False,
                              skip_group_check=True)
                pe.wait_ge(sq_ready, g + 1)
                for j in range(TILES):
                    last = pe.matmul(psS[:, 1:2], sq[:, q % 2, j * F:(j + 1) * F], ones[:, :], start=False,
                                     stop=False, skip_group_check=True)
                last.then_inc(stats_done, 1)

            def edge_step(i):
                for q in range(U):
                    product(i, q)
                    counts(i, q)
                    if q > 0:
                        stats(i, q - 1)
                    elif not (isinstance(i, int) and i == 0):
                        stats(i - 1, U - 1)

            edge_step(0)
            with pe.Fori(1, NI - 1) as i:
                edge_step(i)
            edge_step(NI - 1)
            stats(NI - 1, U - 1)
            pe.wait_ge(s_uin, 1)
            pe.matmul(psT[0][:, 0:F], sq[:, 1, F:2 * F], sq[:, 1, 0:F], start=True, stop=True).then_inc(s_ups, 1)

            def window_sum(i, q):
                g = U * i + q
                pe.wait_ge(m_ready, g + 1)
                pe.wait_ge(hotf_ready, g + 1)
                if not first(i, q, 4):
                    pe.wait_ge(agg_added, g - 3)
                for j in range(TILES):
                    last = pe.matmul(psA[q][:, 0:WIN], mx[:, q, j * F:(j + 1) * F], hotf[:, q, j * WIN:(j + 1) * WIN],
                                     start=(j == 0), stop=(j == TILES - 1))
                last.then_inc(summed, 1)

            pe.wait_ge(cnt_added, NG)
            for q in range(U):
                window_sum(0, q)
            with pe.Fori(1, NI) as i:
                for q in range(U):
                    window_sum(i, q)

            pe.wait_ge(s_nodein, 16 * 11)
            k = 0
            for n, (c0, cw) in enumerate(CHUNKS):
                pe.wait_ge(s_aggm, n + 1)
                for h in range(H2):
                    if k >= 4:
                        pe.wait_ge(s_h2, k - 3)
                    o = BANK[k % 4][:, 0:cw]
                    pe.matmul(o, w2[:, h * P:(h + 1) * P], xt[:, c0:c0 + cw], start=True, stop=False)
                    pe.matmul(o, w2[:, H2 * P + h * P:H2 * P + (h + 1) * P], agg[:, c0:c0 + cw], start=False,
                              stop=True).then_inc(s_h2ps, 1)
                    k += 1
            pe.wait_ge(s_h2r, H2)
            for t in range(NT):
                if t >= 4:
                    pe.wait_ge(s_z, t - 3)
                for h in range(H2):
                    lh = h2r[:, h * N:(h + 1) * N].rearrange("c (p t) -> c t p", t=NT)[:, t, :]
                    last = pe.matmul(BANK[t % 4][0:PN, 0:F], lh, wl[:, h * F:(h + 1) * F], start=(h == 0),
                                     stop=(h == H2 - 1))
                last.then_inc(s_ops, 1)

        @block.scalar
        def _(act):
            act.wait_ge(s_w, 1)
            act.dma_start(w1x[:, :], W1[0:F, :]).then_inc(s_cols, 16)
            act.dma_start(w1e[0:FE, 0, :], W1[F:F + FE, :]).then_inc(s_cols, 16)
            act.dma_start(w1e[FE:P, 1, :], W1[F:F + FE, :]).then_inc(s_cols, 16)
            act.dma_start(gbc, g1.partition_broadcast(P)).then_inc(s_cols, 16)
            for k, v in ((C_G, g1), (C_BE, be1), (C_B1, b1)):
                act.dma_start(c(k), v.rearrange("(p a) -> p a", a=1)).then_inc(s_cols, 16)
            ysv = ysb[0:PN, :].rearrange("p (t f) -> p t f", t=NT)
            for t in range(NT):
                act.wait_ge(s_yps, t + 1)
                act.activation(ysv[:, t, :], psH[t % 2][0:PN, 0:F], ACT.Copy).then_inc(s_ysb, 1)

            def group(i, q):
                g = U * i + q
                act.wait_ge(ea_turned, g + 1)
                if not first(i, q, 2):
                    act.wait_ge(prod_ready, g - 1)
                act.activation(eat[:, q % 2, :], psT[q % 2][:, :], ACT.Copy).then_inc(eat_ready, 1)
                act.wait_ge(h_ready, g + 1)
                if q == KEEP:
                    act.dma_start(spill[bass.ds(i, 1), :, :].rearrange("a p f -> (a p) f"), hs[:, q % 2, :]
                                  ).then_inc(spilled, 16)
                if not first(i, q, 2):
                    act.wait_ge(stats_done, g - 1)
                act.activation(sq[:, q % 2, :], hs[:, q % 2, :], ACT.Square).then_inc(sq_ready, 1)
                if q < KEEP:
                    act.activation(resg(i, q), hs[:, q % 2, :], ACT.Copy).then_inc(kept, 1)

            act.wait_ge(s_idx, 1)
            act.wait_ge(s_tab, 48)
            for q in range(U):
                group(0, q)
            with act.Fori(1, NI) as i:
                for q in range(U):
                    group(i, q)
            act.wait_ge(s_bn1, 4)
            act.activation(c(C_SD), c(C_V), ACT.Sqrt).then_inc(s_sqrt1, 1)

            def stage_loc(i, q):
                if not first(i, q, 4):
                    act.wait_ge(hotf_ready, U * i + q - 3)
                act.activation(locr[:, q, :].unsqueeze(2), loc[:, :, bass.ds(U * i + q, 1)], ACT.Copy
                               ).then_inc(loc_staged, 1)

            for q in range(U):
                stage_loc(0, q)
            with act.Fori(1, NI) as i:
                for q in range(U):
                    stage_loc(i, q)

            k = 0
            for n, (c0, cw) in enumerate(CHUNKS):
                for h in range(H2):
                    act.wait_ge(s_h2ps, k + 1)
                    act.activation(h2[:, h * N + c0:h * N + c0 + cw], BANK[k % 4][:, 0:cw], ACT.Copy
                                   ).then_inc(s_h2, 1)
                    k += 1
            act.wait_ge(s_bn2, 2)
            act.activation(colh[:, 8:10], colh[:, 6:8], ACT.Sqrt).then_inc(s_sqrt2, 1)
            act.wait_ge(s_bn2, 6)
            for h in range(H2):
                act.activation(h2r[:, h * N:(h + 1) * N], h2[:, h * N:(h + 1) * N], ACT.Relu,
                               bias=colh[:, 12 + h:13 + h], scale=colh[:, 10 + h:11 + h]).then_inc(s_h2r, 1)
            act.wait_ge(s_zst, 2)
            act.activation(rs3[0:PN, :], mv3[0:PN, :].rearrange("p (t k) -> p t k", k=2)[:, :, 1], ACT.Sqrt
                           ).then_inc(s_sqrt3, 1)

        @block.vector
        def _(dve):
            chain = [0]

            def link(ins):
                chain[0] += 1
                ins.then_inc(s_dv, 1)
                dve.wait_ge(s_dv, chain[0])

            dve.memset(w1e[:, :, :], 0.0).then_inc(s_w, 1)
            dve.wait_ge(s_rows, 64)
            dve.tensor_copy(srowf[0:NG, :], srow[0:NG, :].bitcast(I32))
            link(dve.tensor_copy(drowf[0:NG, :], drow[0:NG, :].bitcast(I32)))
            dve.tensor_reduce(rowst[0:NG, 0:1], drowf[0:NG, :], AX_X, ALU.min)
            link(dve.tensor_reduce(rowst[0:NG, 1:2], drowf[0:NG, :], AX_X, ALU.max))
            dve.tensor_scalar(drowf[0:NG, :], drowf[0:NG, :], rowst[0:NG, 0:1], None, ALU.subtract).then_inc(s_rowf, 1)
            dve.tensor_tensor(rowst[0:NG, 2:3], rowst[0:NG, 1:2], rowst[0:NG, 0:1], ALU.subtract).then_inc(s_rowf, 1)
            dve.wait_ge(s_cols, 16 * 7)
            link(dve.tensor_scalar(sgn, gbc, 0.0, 2.0, ALU.is_ge, ALU.mult))
            link(dve.tensor_scalar(sgn, sgn, -1.0, None, ALU.add))
            dve.tensor_tensor(w1x[:, :], w1x[:, :], sgn, ALU.mult).then_inc(s_wsgn, 1)
            for a in range(2):
                last = dve.tensor_tensor(w1e[:, a, :], w1e[:, a, :], sgn, ALU.mult)
            last.then_inc(s_wsgn, 1)
            xtv = xt0.rearrange("f (p t) -> f t p", t=NT)
            for t in range(NT):
                dve.wait_ge(s_xps, t + 1)
                dve.tensor_copy(xtv[:, t, :], psC[t % 2][:, 0:PN]).then_inc(s_xt, 1)
            dve.wait_ge(s_rowt, 3)
            dve.tensor_copy(srci[:, :, :].rearrange("p j g -> p (j g)"), psS[:, 0:TILES * NG])
            dve.tensor_copy(loc[:, :, :].rearrange("p j g -> p (j g)"), psX[:, 0:TILES * NG])
            link(dve.tensor_reduce(rowc[0:1, 0:1], psT[1][0:1, 0:NG], AX_X, ALU.max))
            dve.tensor_copy(rowi[0:1, 0:1], rowc[0:1, 0:1])
            link(dve.tensor_copy(basei[0:1, :], psT[0][0:1, 0:NG]))
            dve.memset(col[:, C_M:C_M + 1], 0.0).then_inc(s_idx, 1)

            def onehot_b(i, q):
                g = U * i + q
                if not first(i, q, 2):
                    dve.wait_ge(cnt_ps, g - 1)
                dve.tensor_tensor(hotb[:, q % 2, :].rearrange("p (j w) -> p j w", j=TILES),
                                  iota[:, :].unsqueeze(1).broadcast_to([P, TILES, WIN]),
                                  loc[:, :, bass.ds(g, 1)].broadcast_to([P, TILES, WIN]), ALU.is_equal).then_inc(hotb_ready, 1)

            def add_counts(i, q):
                g = U * i + q
                base = dve.value_load(basei[0:1, bass.ds(g, 1)], min_val=0, max_val=N)
                dve.wait_ge(cnt_ps, g + 1)
                if not first(i, q, 1):
                    dve.wait_ge(cnt_added, g)
                w = cnt[:, bass.ds(base, WIN)]
                dve.tensor_tensor(w, w, psC[q % 2][:, 0:WIN], ALU.add).then_inc(cnt_added, 1)

            def make_h(i, q):
                g = U * i + q
                dve.wait_ge(prod_ready, g + 1)
                dve.wait_ge(gathered[q % 2], 64 * (2 * i + q // 2 + 1))
                if not first(i, q, 2):
                    dve.wait_ge(stats_done, g - 1)
                    if q == 1:
                        dve.wait_ge(spilled, 16 * i)
                    else:
                        dve.wait_ge(kept, {0: 3 * i, 2: 3 * i + 1, 3: 3 * i + 2}[q])
                dve.tensor_tensor(hs[:, q % 2, :], psH[q % 2][:, :], yg[:, q % 2, :], ALU.add).then_inc(h_ready, 1)

            def stage_idx(i, q):
                dve.tensor_copy(idx[:, q, :].unsqueeze(2), srci[:, :, bass.ds(U * i + q, 1)]).then_inc(idx_staged, 1)

            def edge_step(i):
                for q in range(U):
                    onehot_b(i, q)
                    if q > 0:
                        add_counts(i, q - 1)
                    elif not (isinstance(i, int) and i == 0):
                        add_counts(i - 1, U - 1)
                    make_h(i, q)
                    if not (isinstance(i, int) and i == NI - 1):
                        stage_idx(i + 1, q)

            dve.wait_ge(s_set, 1)
            dve.wait_ge(s_idx, 1)
            for q in range(U):
                stage_idx(0, q)
            edge_step(0)
            with dve.Fori(1, NI - 1) as i:
                edge_step(i)
            edge_step(NI - 1)
            add_counts(NI - 1, U - 1)

            def bn(ins):
                bnc[0] += 1
                ins.then_inc(s_bn1, 1)
                dve.wait_ge(s_bn1, bnc[0])

            bnc = [0]
            dve.wait_ge(stats_done, NG)
            bn(dve.tensor_scalar(c(C_M, 2), psS[:, 0:2], 1.0 / E, None, ALU.mult))
            bn(dve.tensor_tensor(c(C_V), c(C_M), c(C_M), ALU.mult))
            bn(dve.tensor_tensor(c(C_V), c(C_Q), c(C_V), ALU.subtract))
            bn(dve.tensor_scalar(c(C_V), c(C_V), 0.0, EPS, ALU.max, ALU.add))
            bn(dve.tensor_scalar(c(C_AG), c(C_G), 0.0, 2.0, ALU.is_ge, ALU.mult))
            bn(dve.tensor_scalar(c(C_AG), c(C_AG), -1.0, None, ALU.add))
            bn(dve.tensor_tensor(c(C_B1), c(C_B1), c(C_AG), ALU.mult))
            bn(dve.tensor_tensor(c(C_AG), c(C_G), c(C_AG), ALU.mult))
            bn(dve.tensor_tensor(c(C_M), c(C_M), c(C_B1), ALU.add))
            bn(dve.tensor_tensor(c(C_M), c(C_B1), c(C_M), ALU.subtract))
            dve.wait_ge(s_sqrt1, 1)
            bn(dve.reciprocal(c(C_R), c(C_SD)))
            bn(dve.tensor_tensor(c(C_S), c(C_AG), c(C_R), ALU.mult))
            bn(dve.tensor_scalar(c(C_S), c(C_S), TINY, None, ALU.max))
            bn(dve.reciprocal(c(C_T), c(C_S)))
            bn(dve.tensor_tensor(c(C_T), c(C_T), c(C_BE), ALU.mult))
            bn(dve.tensor_tensor(c(C_U), c(C_T), c(C_M), ALU.add))
            dve.memset(sq[:, 1, F:2 * F], 1.0)
            dve.tensor_scalar(sq[:, 1, 0:F], ident[:, :], c(C_U), -1.0, ALU.mult, ALU.mult).then_inc(s_uin, 1)
            dve.wait_ge(s_ups, 1)
            dve.tensor_copy(negu[:, :], psT[0][:, 0:F]).then_inc(s_u, 1)
            dve.wait_ge(s_u, 1)

            def maxes(i, q):
                g = U * i + q
                if not first(i, q, 4):
                    dve.wait_ge(summed, g - 3)
                if q < KEEP:
                    hin = resg(i, q)
                else:
                    dve.wait_ge(reload, 16 * (i + 1))
                    hin = back if isinstance(i, int) and i == 0 else resg(i - 1, 0)
                dve.tensor_tensor(mx[:, q, :].rearrange("p (j f) -> p j f", j=TILES),
                                  hin.rearrange("p (j f) -> p j f", j=TILES),
                                  negu[:, :].unsqueeze(1).broadcast_to([P, TILES, F]), ALU.max).then_inc(m_ready, 1)

            def add_window(i, q):
                g = U * i + q
                base = dve.value_load(basei[0:1, bass.ds(g, 1)], min_val=0, max_val=N)
                dve.wait_ge(summed, g + 1)
                if not first(i, q, 1):
                    dve.wait_ge(agg_added, g)
                w = agg[:, bass.ds(base, WIN)]
                dve.tensor_tensor(w, w, psA[q][:, 0:WIN], ALU.add).then_inc(agg_added, 1)

            def sum_step(i):
                for q in range(U):
                    maxes(i, q)
                    if q > 0:
                        add_window(i, q - 1)
                    elif not (isinstance(i, int) and i == 0):
                        add_window(i - 1, U - 1)

            dve.wait_ge(kept, NI * KEEP)
            dve.wait_ge(cnt_added, NG)
            sum_step(0)
            with dve.Fori(1, NI) as i:
                sum_step(i)
            add_window(NI - 1, U - 1)
            dve.wait_ge(agg_added, NG)

            for n, (c0, cw) in enumerate(CHUNKS):
                a, k = agg[:, c0:c0 + cw], cnt[:, c0:c0 + cw]
                t1 = h2r[:, c0:c0 + cw]
                link(dve.tensor_scalar(t1, k, 1.0, None, ALU.max))
                link(dve.reciprocal(t1, t1))
                link(dve.tensor_tensor(a, a, t1, ALU.mult))
                link(dve.tensor_scalar(k, k, 1.0, c(C_U), ALU.min, ALU.mult))
                link(dve.tensor_tensor(a, a, k, ALU.add))
                dve.tensor_scalar(a, a, c(C_S), None, ALU.mult).then_inc(s_aggm, 1)
            k = 0
            bsv = bs2.rearrange("p (h n s) -> p h n s", h=H2, s=6)
            for n, (c0, cw) in enumerate(CHUNKS):
                for h in range(H2):
                    dve.wait_ge(s_h2, k + 1)
                    ins = dve.bn_stats(bsv[:, h, n, :], h2[:, h * N + c0:h * N + c0 + cw])
                    k += 1
            link(ins)
            for h in range(H2):
                last = dve.bn_aggr(mv2[:, 2 * h:2 * h + 2], bsv[:, h, :, :].rearrange("p n s -> p (n s)"))
            bn2 = [0]

            def b2n(ins):
                bn2[0] += 1
                ins.then_inc(s_bn2, 1)
                dve.wait_ge(s_bn2, bn2[0])

            dve.wait_ge(s_nodein, 16 * 11)
            mvv = mv2.rearrange("p (h k) -> p h k", k=2)
            b2n(last)
            b2n(dve.tensor_scalar(colh[:, 6:8], mvv[:, :, 1], EPS, None, ALU.add))
            b2n(dve.tensor_tensor(colh[:, 14:16], mvv[:, :, 0], colh[:, 4:6], ALU.add))
            dve.wait_ge(s_sqrt2, 1)
            b2n(dve.reciprocal(colh[:, 10:12], colh[:, 8:10]))
            link(dve.tensor_tensor(colh[:, 10:12], colh[:, 10:12], colh[:, 0:2], ALU.mult))
            link(dve.tensor_tensor(colh[:, 14:16], colh[:, 4:6], colh[:, 14:16], ALU.subtract))
            b2n(dve.tensor_tensor(colh[:, 12:14], colh[:, 14:16], colh[:, 10:12], ALU.mult))
            b2n(dve.tensor_tensor(colh[:, 12:14], colh[:, 12:14], colh[:, 2:4], ALU.add))
            zv = z[0:PN, :].rearrange("p (t f) -> p t f", t=NT)
            xnv = xn[0:PN, :].rearrange("p (t f) -> p t f", t=NT)
            zov = zo[0:PN, :].rearrange("p (t f) -> p t f", t=NT)
            b3 = bs3[0:PN, :].rearrange("p (t s) -> p t s", s=6)
            m3 = mv3[0:PN, :].rearrange("p (t s) -> p t s", s=2)
            for t in range(NT):
                dve.wait_ge(s_ops, t + 1)
                ins = dve.tensor_tensor(zv[:, t, :], BANK[t % 4][0:PN, 0:F], blr[0:PN, :], ALU.add)
                ins.then_inc(s_z, 1)
            dve.wait_ge(s_z, NT)
            link(dve.scalar_tensor_tensor(out=z[0:PN, :], in0=z[0:PN, :], scalar=0.0, in1=xn[0:PN, :],
                                          op0=ALU.max, op1=ALU.add))
            for t in range(NT):
                ins = dve.bn_stats(b3[:, t, :], zv[:, t, :])
            link(ins)
            for t in range(NT):
                ins = dve.bn_aggr(m3[:, t, :], b3[:, t, :])
            ins.then_inc(s_zst, 1)
            dve.wait_ge(s_zst, 1)
            dve.tensor_scalar(m3[:, :, 1], m3[:, :, 1], EPS, None, ALU.add).then_inc(s_zst, 1)
            dve.wait_ge(s_sqrt3, 1)
            link(dve.reciprocal(rs3[0:PN, :], rs3[0:PN, :]))
            for t in range(NT):
                dve.tensor_scalar(zov[:, t, :], zv[:, t, :], m3[:, t, 0:1], rs3[0:PN, t:t + 1], ALU.subtract,
                                  ALU.mult).then_inc(s_zo, 1)


_INS = ['x', 'src', 'dst', 'edge_attr_64', 'L0_gnn_W1', 'L0_gnn_b1', 'L0_gnn_g1', 'L0_gnn_be1', 'L0_gnn_W2',
        'L0_gnn_b2', 'L0_gnn_g2', 'L0_gnn_be2', 'L0_gnn_Wl', 'L0_gnn_bl']


def kernel(**inputs):
    import numpy as np
    import concourse.bacc as bacc
    from concourse.bass_utils import run_bass_kernel_spmd as run

    nc = bacc.Bacc("TRN2", target_bir_lowering=False, num_devices=1)
    arrays, args = {}, []
    for name in _INS:
        a = np.ascontiguousarray(inputs[name])
        arrays[f"in_{name}"] = a
        args.append(nc.dram_tensor(f"in_{name}", a.shape, mybir.dt.from_np(a.dtype), kind="ExternalInput").ap())
    shape = inputs['x'].shape
    args.append(nc.dram_tensor("out_dram", shape, F32, kind="ExternalOutput").ap())
    gnn_kernel(nc, *args)
    r = run(nc, [arrays], core_ids=[0])
    return r.results[0]["out_dram"]
```

```python
from contextlib import ExitStack

import concourse.bass as bass
from concourse import mybir

F32 = mybir.dt.float32
BF16 = mybir.dt.bfloat16
I32 = mybir.dt.int32
ALU = mybir.AluOpType
ACT = mybir.ActivationFunctionType
AX_X = mybir.AxisListType.X

P = 128
EPS = 1e-5
TINY = 1e-20
TILES = 4
GROUP = TILES * P
U = 4
KEEP = 3
WIN = 64
BEYOND = 64
WIDE = 256


def gnn_kernel(nc, x, src, dst, ea, W1, b1, g1, be1, W2, b2, g2, be2, Wl, bl, out):
    N, F = x.shape
    E, FE = ea.shape
    H2 = W2.shape[1] // P
    NT = 25
    PN = N // NT
    NG = (E + GROUP - 1) // GROUP
    NI = NG // U
    assert F == P and FE * 2 == P and NT * PN == N and NG == NI * U and H2 == 2
    LAST = E - (NG - 1) * GROUP
    LP = LAST // TILES
    LR = LAST - LP * TILES
    PAD = N
    YROWS = 25 * P
    NB = (N + WIDE) // WIDE
    NAGG = NB * WIDE
    assert NAGG >= N + WIN and NI % 2 == 0
    CH = 4 * PN
    CHUNKS = [(c, min(CH, N - c)) for c in range(0, N, CH)]
    NC = len(CHUNKS)
    BATCH = [(t, min(4, NT - t)) for t in range(0, NT, 4)]

    ytab = nc.dram_tensor("ytab", (YROWS, F), F32, kind="Internal").ap()
    xt_dram = nc.dram_tensor("xt_dram", (P, N), F32, kind="Internal").ap()
    spill = nc.dram_tensor("spill", (NI, P, TILES * F), F32, kind="Internal").ap()
    rc_dram = nc.dram_tensor("rc_dram", (N,), F32, kind="Internal").ap()
    hot_dram = nc.dram_tensor("hot_dram", (NI, P, U * TILES * WIN), BF16, kind="Internal").ap()

    ctx = ExitStack()
    with ctx:
        def sb(name, shape, dt=F32):
            return ctx.enter_context(nc.sbuf_tensor(name, shape, dt))

        def pb(name, shape):
            return ctx.enter_context(nc.psum_tensor(name, shape, F32))

        def sem(name):
            return ctx.enter_context(nc.semaphore(name))

        GF = TILES * F
        res = sb("res", [P, NI * KEEP * GF])
        work = sb("work", [P, 6, GF])
        yg = work[:, 0:2, :]
        hs = work[:, 2:4, :]
        sq = work[:, 4:6, :]
        mx = work[:, 0:4, :]
        back = work[:, 4, :]
        work2 = sb("work2", [P, 4, TILES * WIN])
        ear = work2[:, 0:2, :]
        eat = work2[:, 2:4, :]
        hotf = work2
        hotb = sb("hotb", [P, U, TILES * WIN], BF16)
        hotb2 = work[:, 5, :].bitcast(BF16).rearrange("p (q w) -> p q w", q=U)
        agg = sb("agg", [P, NAGG])
        cnt = sb("cnt", [P, NAGG])
        srci = sb("srci", [P, TILES, NG], I32)
        idx = sb("idx", [P, U, TILES], I32)
        loc = sb("loc", [P, TILES, NG])
        basei = sb("basei", [1, NG], I32)
        ident = sb("ident", [P, P])
        w1x = sb("w1x", [P, F])
        w1e = sb("w1e", [P, 2, F])
        iota = sb("iota", [P, WIN])
        ones = sb("ones", [P, 1])
        onesb = sb("onesb", [P, P], BF16)
        zero2 = sb("zero2", [P, 2])
        col = sb("col", [P, 24])
        cntc = sb("cntc", [P, NT])
        rowc = sb("rowc", [1, 4])
        rowi = sb("rowi", [1, 4], I32)

        TAB = 16 * (len(BATCH) + 1)
        ghot = work2[:, :, :].rearrange("p q w -> p (q w)")
        wsum = srci[:, :, :].rearrange("p j g -> p (j g)").bitcast(F32)[:, 0:U * WIN].rearrange(
            "p (q w) -> p q w", q=U)
        giota = hotb[:, :, :].rearrange("p q w -> p (q w)").bitcast(F32)

        at = NI * KEEP * GF

        def tail(n):
            nonlocal at
            at -= n
            return res[:, at:at + n]

        xn0 = tail(NT * F)
        ysb = tail(NT * F)
        xt0 = tail(N)
        srow = tail(GROUP)
        drow = tail(GROUP)
        srowf = tail(GROUP)
        drowf = tail(GROUP)
        rowst = tail(4)
        zeros = tail(F)
        sgn = tail(F)
        gbc = tail(F)

        near = 0

        def head(n):
            nonlocal near
            near += n
            return res[:, near - n:near]

        xt = head(N)
        xn = head(NT * F)
        w2 = head(2 * H2 * P)
        wl = head(H2 * F)
        blr = head(F)
        zo = head(NT * F)
        h2 = head(H2 * N)
        h2r = head(H2 * N)
        z = head(NT * F)
        bs2 = head(H2 * NC * 6)
        bs3 = head(NT * 6)
        mv3 = head(NT * 2)
        rs3 = head(NT)
        nm3 = head(NT)
        colh = head(16)
        mv2 = head(2 * H2)

        psT = [pb(f"psT{i}", [P, 512]) for i in range(2)]
        psH = [pb(f"psH{i}", [P, GF]) for i in range(2)]
        psC = [pb(f"psC{i}", [P, GF]) for i in range(2)]
        psS = pb("psS", [P, 512])
        psX = pb("psX", [P, 512])
        psA = [psH[0], psH[1], psC[0], psC[1]]

        negu = psX[:, :]
        BANK = [psT[0], psT[1], psS] + psA

        s_x = [sem(f"x_loaded{b}") for b in range(len(BATCH))]
        s_w = sem("w_loaded")
        s_rowset = sem("rows_preset")
        s_rows = sem("rows_loaded")
        s_cols = sem("cols_loaded")
        s_ident = sem("ident_ready")
        s_pool = sem("pool_chain")
        s_wsgn = sem("w1_signed")
        s_dv = sem("dve_chain")
        s_rowf = sem("rows_as_float")
        s_rowt = sem("rows_turned")
        s_idx = sem("indices_ready")
        s_xps = sem("x_turned_psum")
        s_xt = sem("xt_ready")
        s_yps = sem("y_psum")
        s_ysb = sem("y_ready")
        s_zr = sem("zeros_ready")
        s_tab = sem("table_written")
        s_xtd = sem("xt_saved")
        ea_loaded = [sem(f"ea_loaded{i}") for i in range(2)]
        ea_turned = sem("ea_turned")
        eat_ready = sem("eat_ready")
        prod_ready = sem("ea_product_ready")
        idx_staged = sem("idx_staged")
        gathered = [sem(f"gathered{i}") for i in range(2)]
        h_ready = sem("h_ready")
        sq_ready = sem("sq_ready")
        h_summed = sem("h_summed")
        sq_summed = sem("sq_summed")
        s_folded = sem("sums_folded")
        kept = sem("kept")
        spilled = sem("spilled")
        hotb_ready = sem("hotb_ready")
        cnt_ps = sem("cnt_psum_ready")
        cnt_added = sem("cnt_added")
        s_set = sem("memory_preset")
        s_bn1 = sem("bn1_chain")
        s_sqrt1 = sem("bn1_sqrt")
        s_uin = sem("diag_u_ready")
        s_ups = sem("u_spread")
        s_u = sem("negu_ready")
        reload = sem("group_back")
        slot_passed = sem("slot_passed")
        hot_saved = sem("hot_saved")
        hot_back = [sem(f"hot_back{i}") for i in range(2)]
        sums_over = sem("sums_over")
        s_masked = sem("edgeless_marked")
        s_cc = sem("counts_compact")
        s_rc = sem("reciprocals_ready")
        s_rcd = sem("reciprocals_in_dram")
        s_rcb = sem("reciprocals_spread")
        g_base = sem("general_base_spread")
        g_back = sem("general_group_back")
        g_m = sem("general_max_ready")
        g_iota = sem("general_iota_ready")
        g_hot = sem("general_hot_ready")
        g_summed = sem("general_summed")
        g_added = sem("general_added")
        hotf_ready = sem("hotf_ready")
        m_ready = sem("max_ready")
        summed = sem("window_summed")
        agg_set = sem("agg_preset")
        wsum_ready = sem("window_copied")
        agg_added = sem("agg_added")
        s_nodein = sem("node_inputs_loaded")
        s_tail = sem("tail_chain")
        s_aggm = sem("mean_ready")
        s_h2ps = sem("h2_psum")
        s_h2 = sem("h2_copied")
        s_h2st = sem("h2_stats")
        s_bn2 = sem("bn2_chain")
        s_sqrt2 = sem("bn2_sqrt")
        s_h2r = sem("h2_relu")
        s_ops = sem("out_psum")
        s_z = sem("z_ready")
        s_zst = sem("z_stats")
        s_sqrt3 = sem("ln_sqrt")
        s_ln = sem("ln_scale_ready")
        s_bl = sem("bl_added")
        s_zo = sem("out_rows_ready")
        s_out = sem("out_written")

        C_SUM, C_G, C_BE, C_B1, C_M, C_Q, C_V, C_SD, C_R, C_S, C_T, C_U, C_AG, C_SU = range(14)

        def c(i, n=1):
            return col[:, i:i + n]

        def resg(i, q):
            return res[:, bass.ds((i * KEEP + q) * GF, GF)]

        def first(i, q, back_by):
            return isinstance(i, int) and U * i + q < back_by

        def h2_copy(act, k):
            n, h = k // H2, k % H2
            c0, cw = CHUNKS[n]
            act.wait_ge(s_h2ps, k + 1)
            act.activation(h2[:, h * N + c0:h * N + c0 + cw], BANK[k % len(BANK)][:, 0:cw], ACT.Copy
                           ).then_inc(s_h2, 1)

        def normalise(act, b, zv, zov):
            t0, n = BATCH[b]
            act.wait_ge(s_ln, b + 1)
            for t in range(t0, t0 + n):
                act.activation(zov[:, t, :], zv[:, t, :], ACT.Identity, bias=nm3[0:PN, t:t + 1],
                               scale=rs3[0:PN, t:t + 1]).then_inc(s_zo, 1)

        def spread_counts(q):
            q.wait_ge(s_masked, 1)
            q.dma_start(cntc[0:PN, :], cnt[0:1, 0:N]).then_inc(s_cc, 16)
            q.wait_ge(s_rc, 2)
            q.dma_start(rc_dram.rearrange("(p t) -> p t", t=NT), cntc[0:PN, :]).then_inc(s_rcd, 16)
            q.wait_ge(s_rcd, 16)
            q.dma_start(cnt[:, 0:N], rc_dram.partition_broadcast(P)).then_inc(s_rcb, 16)

        def invert_counts(dve):
            dve.wait_ge(s_cc, 16)
            dve.tensor_scalar(cntc[0:PN, :], cntc[0:PN, :], 1.0, None, ALU.max).then_inc(s_rc, 1)
            dve.wait_ge(s_rc, 1)
            dve.reciprocal(cntc[0:PN, :], cntc[0:PN, :]).then_inc(s_rc, 1)

        def general(dve, resg):
            iota0, now = giota[:, 0:WIDE], giota[:, WIDE:2 * WIDE]
            dve.tensor_copy(work[0:1, 2, 0:NG], basei[0:1, :]).then_inc(g_base, 1)
            dve.memset(agg[:, :], 0.0)
            dve.memset(cnt[:, :], 0.0)
            dve.wait_ge(hot_saved, 16 * NI)
            for k in range(WIDE // WIN):
                dve.tensor_scalar(giota[:, k * WIN:(k + 1) * WIN], iota[:, :], float(k * WIN), None, ALU.add)
            dve.wait_ge(g_base, 2)
            dve.tensor_tensor(loc[:, :, :], loc[:, :, :],
                              psT[0][:, 0:NG].unsqueeze(1).broadcast_to([P, TILES, NG]), ALU.add).then_inc(g_iota, 1)
            with dve.Fori(0, NI) as i:
                for q in range(U):
                    g = U * i + q
                    if q == KEEP:
                        dve.wait_ge(g_back, 16 * (i + 1))
                    dve.tensor_tensor(mx[:, 0, :], resg(i, q) if q < KEEP else back, negu, ALU.max).then_inc(g_m, 1)
                    dve.wait_ge(g_iota, (NB + 1) * g + 1)
                    dve.tensor_copy(now, iota0).then_inc(g_iota, 1)
                    with dve.Fori(0, NB) as b:
                        dve.wait_ge(g_iota, (NB + 1) * g + b + 2)
                        for j in range(TILES):
                            last = dve.tensor_scalar(ghot[:, j * WIDE:(j + 1) * WIDE], now,
                                                     loc[:, j, bass.ds(g, 1)], None, ALU.is_equal)
                        last.then_inc(g_hot, 1)
                        dve.wait_ge(g_hot, NB * g + b + 1)
                        dve.tensor_scalar(now, now, float(WIDE), None, ALU.add).then_inc(g_iota, 1)
                        dve.wait_ge(g_summed, NB * g + b + 1)
                        a = agg[:, bass.ds(b * WIDE, WIDE)]
                        n = cnt[:, bass.ds(b * WIDE, WIDE)]
                        dve.tensor_tensor(a, a, psH[0][:, 0:WIDE], ALU.add)
                        dve.tensor_tensor(n, n, psH[1][:, 0:WIDE], ALU.add).then_inc(g_added, 1)
                        dve.wait_ge(g_added, NB * g + b + 1)
            none = res[:, NI * KEEP * GF - NAGG:NI * KEEP * GF]
            dve.tensor_scalar(none, cnt[:, :], 0.0, None, ALU.is_equal).then_inc(g_added, 1)
            dve.wait_ge(g_added, NB * NG + 1)
            dve.sem_inc(s_masked, 1)
            dve.tensor_scalar(none, none, c(C_U), -1.0, ALU.mult, ALU.mult).then_inc(g_added, 1)
            dve.wait_ge(g_added, NB * NG + 2)
            dve.tensor_tensor(agg[:, :], agg[:, :], none, ALU.add)
            invert_counts(dve)
            dve.drain().then_inc(sums_over, 1)

        block = ctx.enter_context(nc.Block())

        @block.sync
        def _(sp):
            xv = x.rearrange("(p t) f -> p t f", t=NT)
            xnv = xn0[0:PN, :].rearrange("p (t f) -> p t f", t=NT)
            for b, (t, n) in enumerate(BATCH):
                sp.dma_start(xnv[:, t:t + n, :], xv[:, t:t + n, :]).then_inc(s_x[b], 16)
            sp.wait_ge(s_zr, 1)
            sp.dma_start(ytab[N:YROWS, :], zeros[0:YROWS - N, :]).then_inc(s_tab, 16)
            yv = ytab[0:N, :].rearrange("(p t) f -> p t f", t=NT)
            ysv = ysb[0:PN, :].rearrange("p (t f) -> p t f", t=NT)
            for b, (t, n) in enumerate(BATCH):
                sp.wait_ge(s_ysb, b + 1)
                sp.dma_start(yv[:, t:t + n, :], ysv[:, t:t + n, :]).then_inc(s_tab, 16)
            sp.wait_ge(s_xt, len(BATCH))
            sp.dma_start(xt_dram, xt0[:, :]).then_inc(s_xtd, 16)

            def load_ea(i, q):
                if not first(i, q, 2):
                    sp.wait_ge(ea_turned, U * i + q - 1)
                s = ea_loaded[q % 2]
                sp.dma_start(ear[:, q % 2, :],
                             ea[bass.ds((i * U + q) * GROUP, GROUP), :].rearrange(
                                 "(p j) f -> p (j f)", j=TILES)).then_inc(s, 16)

            for q in range(U):
                load_ea(0, q)
            with sp.Fori(1, NI - 1) as i:
                for q in range(U):
                    load_ea(i, q)
            for q in range(U - 1):
                load_ea(NI - 1, q)
            sp.wait_ge(ea_turned, NG - 2)
            sp.wait_ge(s_tab, TAB)
            e0 = (NG - 1) * GROUP
            s = ea_loaded[1]
            sp.dma_start(ear[0:LP, 1, :],
                         ea[e0:e0 + LP * TILES, :].rearrange("(p j) f -> p (j f)", j=TILES)).then_inc(s, 16)
            sp.dma_start(ear[LP:LP + 1, 1, 0:LR * FE],
                         ea[e0 + LP * TILES:E, :].rearrange("(p j) f -> p (j f)", p=1)).then_inc(s, 16)
            zr = ytab[N:YROWS, :].rearrange("r f -> (r f)")
            n1 = (TILES - LR) * FE
            sp.dma_start(ear[LP:LP + 1, 1, LR * FE:],
                         zr[0:n1].rearrange("(p f) -> p f", p=1)).then_inc(s, 16)
            n2 = (P - LP - 1) * TILES * FE
            sp.dma_start(ear[LP + 1:P, 1, :],
                         zr[n1:n1 + n2].rearrange("(p f) -> p f", f=TILES * FE)).then_inc(s, 16)

            sp.wait_ge(spilled, 16 * NI)
            sp.wait_ge(hot_saved, 16 * NI)
            sp.wait_ge(s_folded, 2)
            wide = sp.value_load(rowi[0:1, 0:1], min_val=0, max_val=N)

            def load_hot(i, par):
                sp.dma_start((hotb, hotb2)[par][:, :, :].rearrange("p q w -> p (q w)"),
                             hot_dram[bass.ds(i, 1), :, :].rearrange("a p w -> (a p) w")
                             ).then_inc(hot_back[par], 16)

            def load_back(i, ahead):
                sp.wait_ge(m_ready, U * i + 1)
                sp.sem_inc(slot_passed, 1)
                sp.wait_ge(reload, 16 * (i + 1))
                sp.sem_inc(slot_passed, 1)
                sp.dma_start(resg(i, 0), spill[bass.ds(i + 1, 1), :, :].rearrange("a p f -> (a p) f")
                             ).then_inc(reload, 16)

            with sp.If(wide < WIN):
                load_hot(0, 0)
                sp.dma_start(back, spill[0, :, :]).then_inc(reload, 16)
                load_hot(1, 1)
                load_back(0, 1)
                spread_counts(sp)
                with sp.Fori(1, NI // 2) as k:
                    for par in range(2):
                        sp.wait_ge(hotf_ready, U * (2 * k + par - 1))
                        sp.sem_inc(slot_passed, 1)
                        load_hot(2 * k + par, par)
                        load_back(2 * k + par - 1, 1)
            with sp.Else():
                sp.dma_start(back, spill[0, :, :]).then_inc(g_back, 16)
                with sp.Fori(1, NI) as i:
                    sp.wait_ge(g_m, U * i)
                    sp.sem_inc(slot_passed, 1)
                    sp.dma_start(back, spill[bass.ds(i, 1), :, :].rearrange("a p f -> (a p) f")
                                 ).then_inc(g_back, 16)
                sp.wait_ge(g_m, NG)
                spread_counts(sp)
            sp.dma_start(xt, xt_dram).then_inc(s_nodein, 16)
            sp.dma_start(xn[0:PN, :], x.rearrange("(p t) f -> p (t f)", t=NT)).then_inc(s_nodein, 16)
            sp.dma_start(w2.rearrange("p (k c) -> p k c", k=2), W2.rearrange("(k p) c -> p k c", k=2)
                         ).then_inc(s_nodein, 16)
            sp.dma_start(wl.rearrange("p (k c) -> p k c", k=H2), Wl.rearrange("(k p) c -> p k c", k=H2)
                         ).then_inc(s_nodein, 16)
            sp.dma_start(blr[0:PN, :], bl.partition_broadcast(PN)).then_inc(s_nodein, 16)
            for k, v in enumerate((g2, be2, b2)):
                for h in range(H2):
                    sp.dma_start(colh[:, 2 * k + h:2 * k + h + 1],
                                 v[h * P:(h + 1) * P].rearrange("(p a) -> p a", a=1)).then_inc(s_nodein, 16)
            ov = out.rearrange("(p t) f -> p t f", t=NT)
            zov = zo[0:PN, :].rearrange("p (t f) -> p t f", t=NT)
            for t, n in BATCH:
                sp.wait_ge(s_zo, t + n)
                sp.dma_start(ov[:, t:t + n, :], zov[:, t:t + n, :]).then_inc(s_out, 16)
            sp.wait_ge(s_out, 16 * len(BATCH))

        @block.gpsimd
        def _(pool):
            pool.memset(srow.bitcast(I32), PAD)
            pool.memset(drow.bitcast(I32), PAD).then_inc(s_rowset, 1)
            pool.memset(ident[:, :], 0.0).then_inc(s_pool, 1)
            pool.wait_ge(s_pool, 1)
            pool.affine_select(out=ident[:, :], in_=ident[:, :], compare_op=ALU.not_equal, fill=1.0, base=0,
                               pattern=[[-1, P]], channel_multiplier=1).then_inc(s_ident, 1)
            pool.memset(zeros, 0.0).then_inc(s_zr, 1)
            pool.iota(iota[:, :], [[1, WIN]], base=0, channel_multiplier=0,
                      allow_small_or_imprecise_dtypes=True)
            pool.memset(onesb[:, :], 1.0)
            pool.memset(ones[:, :], 1.0)
            pool.memset(zero2[:, :], 0.0)
            pool.memset(cnt[:, :], 0.0)
            pool.drain().then_inc(s_set, 1)
            pool.wait_ge(s_idx, 1)
            pool.wait_ge(s_tab, TAB)

            def gather(i, q):
                if not first(i, q, 2):
                    pool.wait_ge(h_ready, U * i + q - 1)
                pool.wait_ge(idx_staged, U * i + q + 1)
                pool.sem_inc(slot_passed, 1)
                for j in range(TILES):
                    pool.indirect_dma_start(
                        yg[:, q % 2, j * F:(j + 1) * F], None, ytab,
                        bass.IndirectOffsetOnAxis(ap=idx[:, q, j:j + 1], axis=0)
                    ).then_inc(gathered[q % 2], 16)

            for q in range(U):
                gather(0, q)
            with pool.Fori(1, NI) as i:
                for q in range(U):
                    gather(i, q)

            def add_window(i, q):
                g = U * i + q
                base = pool.value_load(basei[0:1, bass.ds(g, 1)], min_val=0, max_val=N)
                pool.wait_ge(wsum_ready, g + 1)
                if not first(i, q, 1):
                    pool.wait_ge(agg_added, g)
                w = agg[:, bass.ds(base, WIN)]
                pool.tensor_tensor(w, w, wsum[:, q, :], ALU.add).then_inc(agg_added, 1)

            wide = pool.value_load(rowi[0:1, 0:1], min_val=0, max_val=N)
            pool.wait_ge(agg_set, 1)
            with pool.If(wide < WIN):
                for q in range(U):
                    add_window(0, q)
                with pool.Fori(1, NI) as i:
                    for q in range(U):
                        add_window(i, q)
                pool.wait_ge(agg_added, NG)
                pool.drain().then_inc(sums_over, 1)

        @block.tensor
        def _(pe):
            pe.wait_ge(s_ident, 1)
            pe.wait_ge(s_rowf, 2)
            for k, r in enumerate((srowf, drowf)):
                rv = r[0:NG, :].rearrange("g (p j) -> g j p", j=TILES)
                for j in range(TILES):
                    last = pe.transpose((psS, psX)[k][:, j * NG:(j + 1) * NG], rv[:, j, :], ident[0:NG, 0:NG])
                last.then_inc(s_rowt, 1)
            pe.transpose(psT[0][0:1, 0:NG], rowst[0:NG, 0:1], ident[0:NG, 0:NG])
            pe.transpose(psT[1][0:1, 0:NG], rowst[0:NG, 2:3], ident[0:NG, 0:NG]).then_inc(s_rowt, 1)
            xv = xn0[0:PN, :].rearrange("p (t f) -> p t f", t=NT)
            xtv = xt0.rearrange("f (p t) -> f t p", t=NT)

            def turn_x(b):
                t0, n = BATCH[b]
                pe.wait_ge(s_x[b], 16)
                if b >= 2:
                    pe.wait_ge(s_xt, b - 1)
                for t in range(n):
                    last = pe.transpose(psC[b % 2][:, t * PN:(t + 1) * PN], xv[:, t0 + t, :], ident[0:PN, 0:PN])
                last.then_inc(s_xps, 1)

            turn_x(0)
            for b, (t0, n) in enumerate(BATCH):
                if b + 1 < len(BATCH):
                    turn_x(b + 1)
                pe.wait_ge(s_xt, b + 1)
                if b == 0:
                    pe.wait_ge(s_wsgn, 2)
                if b >= 2:
                    pe.wait_ge(s_ysb, b - 1)
                for t in range(n):
                    last = pe.matmul(psH[b % 2][0:PN, t * F:(t + 1) * F], xtv[:, t0 + t, :], w1x[:, :],
                                     start=True, stop=True)
                last.then_inc(s_yps, 1)
            pe.wait_ge(s_idx, 1)
            pe.wait_ge(s_set, 1)
            def product(i, q):
                g = U * i + q
                pe.wait_ge(ea_loaded[q % 2], 16 * (2 * i + q // 2 + 1) if not (isinstance(i, int) and g == NG - 1)
                           else 16 * (2 * i + q // 2 + 4))
                if not first(i, q, 2):
                    pe.wait_ge(eat_ready, g - 1)
                for b in range(2):
                    last = pe.transpose(psT[q % 2][:, b * P:(b + 1) * P], ear[:, q % 2, b * P:(b + 1) * P], ident[:, :])
                last.then_inc(ea_turned, 1)
                pe.wait_ge(eat_ready, g + 1)
                if not first(i, q, 2):
                    pe.wait_ge(h_ready, g - 1)
                for b in range(2):
                    last = pe.matmul(psH[q % 2][:, b * 2 * F:(b + 1) * 2 * F], eat[:, q % 2, b * P:(b + 1) * P],
                                     w1e[:, :, :].rearrange("p a f -> p (a f)"), start=True, stop=True)
                last.then_inc(prod_ready, 1)

            def counts(i, q):
                g = U * i + q
                pe.wait_ge(hotb_ready, g + 1)
                if not first(i, q, 2):
                    pe.wait_ge(cnt_added, g - 1)
                for j in range(TILES):
                    last = pe.matmul(psC[q % 2][:, 0:WIN], onesb[:, :], hotb[:, q, j * WIN:(j + 1) * WIN],
                                     start=(j == 0), stop=(j == TILES - 1))
                last.then_inc(cnt_ps, 1)

            def edge_step(i):
                for q in range(U):
                    product(i, q)
                    counts(i, q)

            edge_step(0)
            with pe.Fori(1, NI - 1) as i:
                edge_step(i)
            edge_step(NI - 1)
            pe.wait_ge(s_folded, 1)
            pe.matmul(psT[0][:, 0:1], sq[:, 0, 0:F], ones[:, :], start=True, stop=True)
            pe.matmul(psT[0][:, 1:2], sq[:, 0, F:2 * F], ones[:, :], start=True, stop=True).then_inc(s_folded, 1)
            pe.wait_ge(s_uin, 1)
            for j in range(TILES):
                last = pe.matmul(negu[:, j * F:(j + 1) * F], work[:, 3, F:2 * F], work[:, 3, 0:F], start=True,
                                 stop=True)
            last.then_inc(s_ups, 1)
            wide = pe.value_load(rowi[0:1, 0:1], min_val=0, max_val=N)

            def window_sum(i, q):
                g = U * i + q
                pe.wait_ge(m_ready, g + 1)
                pe.wait_ge(hotf_ready, g + 1)
                if not first(i, q, 4):
                    pe.wait_ge(wsum_ready, g - 3)
                for j in range(TILES):
                    n = min(WIN + BEYOND, (TILES - j) * WIN)
                    last = pe.matmul(psA[q][:, 0:n], mx[:, q, j * F:(j + 1) * F], hotf[:, q, j * WIN:j * WIN + n],
                                     start=(j == 0), stop=(j == TILES - 1))
                last.then_inc(summed, 1)

            pe.wait_ge(cnt_added, NG)
            with pe.If(wide < WIN):
                for q in range(U):
                    window_sum(0, q)
                with pe.Fori(1, NI) as i:
                    for q in range(U):
                        window_sum(i, q)
            with pe.Else():
                pe.wait_ge(g_base, 1)
                pe.matmul(psT[0][:, 0:NG], work[0:1, 3, F:2 * F], work[0:1, 2, 0:NG], start=True,
                          stop=True).then_inc(g_base, 1)
                with pe.Fori(0, NG) as g:
                    with pe.Fori(0, NB) as b:
                        pe.wait_ge(g_m, g + 1)
                        pe.wait_ge(g_hot, NB * g + b + 1)
                        for j in range(TILES):
                            pe.matmul(psH[0][:, 0:WIDE], mx[:, 0, j * F:(j + 1) * F], ghot[:, j * WIDE:(j + 1) * WIDE],
                                      start=(j == 0), stop=(j == TILES - 1))
                        for j in range(TILES):
                            last = pe.matmul(psH[1][:, 0:WIDE], work[:, 3, F:2 * F],
                                             ghot[:, j * WIDE:(j + 1) * WIDE], start=(j == 0), stop=(j == TILES - 1))
                        last.then_inc(g_summed, 1)

            pe.wait_ge(s_nodein, 16 * 11)
            prods = [(n, h) for n in range(NC) for h in range(H2)]

            def x_part(k):
                n, h = prods[k]
                c0, cw = CHUNKS[n]
                if k >= len(BANK):
                    pe.wait_ge(s_h2, k - len(BANK) + 1)
                pe.matmul(BANK[k % len(BANK)][:, 0:cw], w2[:, h * P:(h + 1) * P], xt[:, c0:c0 + cw], start=True,
                          stop=False)

            for k in range(3):
                x_part(k)
            for k, (n, h) in enumerate(prods):
                c0, cw = CHUNKS[n]
                pe.wait_ge(s_aggm, n + 1)
                pe.matmul(BANK[k % len(BANK)][:, 0:cw], w2[:, H2 * P + h * P:H2 * P + (h + 1) * P],
                          agg[:, c0:c0 + cw], start=False, stop=True).then_inc(s_h2ps, 1)
                if k + 3 < len(prods):
                    x_part(k + 3)
            pe.wait_ge(s_h2, len(prods))
            pe.wait_ge(s_h2r, H2)
            for b, (t0, n) in enumerate(BATCH):
                if b >= 4:
                    pe.wait_ge(s_z, b - 3)
                for t in range(n):
                    o = BANK[b % 4][0:PN, t * F:(t + 1) * F]
                    for h in range(H2):
                        lh = h2r[:, h * N:(h + 1) * N].rearrange("c (p t) -> c t p", t=NT)[:, t0 + t, :]
                        last = pe.matmul(o, lh, wl[:, h * F:(h + 1) * F], start=(h == 0), stop=(h == H2 - 1))
                last.then_inc(s_ops, 1)

        @block.scalar
        def _(act):
            act.wait_ge(s_w, 1)
            act.dma_start(w1x[:, :], W1[0:F, :]).then_inc(s_cols, 16)
            act.dma_start(gbc, g1.partition_broadcast(P)).then_inc(s_cols, 16)
            act.wait_ge(s_rowset, 1)
            for r, d in ((srow, src), (drow, dst)):
                act.dma_start(r[0:NG - 1, :].bitcast(I32),
                              d[0:(NG - 1) * GROUP].rearrange("(g e) -> g e", e=GROUP)).then_inc(s_rows, 16)
                act.dma_start(r[NG - 1:NG, 0:LAST].bitcast(I32),
                              d[(NG - 1) * GROUP:E].rearrange("(g e) -> g e", g=1)).then_inc(s_rows, 16)
            act.dma_start(w1e[0:FE, 0, :], W1[F:F + FE, :]).then_inc(s_cols, 16)
            act.dma_start(w1e[FE:P, 1, :], W1[F:F + FE, :]).then_inc(s_cols, 16)
            for k, v in ((C_G, g1), (C_BE, be1), (C_B1, b1)):
                act.dma_start(c(k), v.rearrange("(p a) -> p a", a=1)).then_inc(s_cols, 16)
            for b, (t, n) in enumerate(BATCH):
                act.wait_ge(s_yps, b + 1)
                act.activation(ysb[0:PN, t * F:(t + n) * F], psH[b % 2][0:PN, 0:n * F], ACT.Copy).then_inc(s_ysb, 1)

            def turned(i, q):
                g = U * i + q
                act.wait_ge(ea_turned, g + 1)
                if not first(i, q, 2):
                    act.wait_ge(prod_ready, g - 1)
                act.activation(eat[:, q % 2, :], psT[q % 2][:, 0:2 * P], ACT.Copy).then_inc(eat_ready, 1)

            def store(i, q):
                g = U * i + q
                act.wait_ge(h_ready, g + 1)
                if q == KEEP:
                    act.dma_start(spill[bass.ds(i, 1), :, :].rearrange("a p f -> (a p) f"), hs[:, q % 2, :]
                                  ).then_inc(spilled, 16)
                elif q == KEEP - 1:
                    act.wait_ge(hotb_ready, U * i + U)
                    act.dma_start(hot_dram[bass.ds(i, 1), :, :].rearrange("a p w -> (a p) w"),
                                  hotb[:, :, :].rearrange("p q w -> p (q w)")).then_inc(hot_saved, 16)
                if not first(i, q, 2):
                    act.wait_ge(sq_summed, g - 1)
                act.activation(sq[:, q % 2, :], hs[:, q % 2, :], ACT.Square).then_inc(sq_ready, 1)
                if q < KEEP:
                    act.activation(resg(i, q), hs[:, q % 2, :], ACT.Copy).then_inc(kept, 1)

            def edge_step(i):
                for q in range(U):
                    if q < U - 1:
                        turned(i, q + 1)
                    elif not (isinstance(i, int) and i == NI - 1):
                        turned(i + 1, 0)
                    store(i, q)

            act.wait_ge(s_idx, 1)
            turned(0, 0)
            edge_step(0)
            act.wait_ge(s_xtd, 16)
            act.wait_ge(s_tab, TAB)
            with act.Fori(1, NI - 1) as i:
                edge_step(i)
            edge_step(NI - 1)
            act.wait_ge(s_bn1, 4)
            act.activation(c(C_SD), c(C_V), ACT.Sqrt).then_inc(s_sqrt1, 1)
            wide = act.value_load(rowi[0:1, 0:1], min_val=0, max_val=N)

            def hot_rows(i, q, par, uses):
                g = U * i + q
                if q == 0:
                    act.wait_ge(hot_back[par], 16 * uses)
                if not first(i, q, 4):
                    act.wait_ge(summed, g - 3)
                act.activation(hotf[:, q, :], (hotb, hotb2)[par][:, q, :], ACT.Copy).then_inc(hotf_ready, 1)

            def window_out(i, q):
                g = U * i + q
                act.wait_ge(summed, g + 1)
                if not first(i, q, 4):
                    act.wait_ge(agg_added, g - 3)
                act.activation(wsum[:, q, :], psA[q][:, 0:WIN], ACT.Copy).then_inc(wsum_ready, 1)

            def spread_step(i, par, uses):
                for q in range(U):
                    hot_rows(i, q, par, uses)
                    if q >= 2:
                        window_out(i, q - 2)
                    elif not (isinstance(i, int) and i == 0):
                        window_out(i - 1, q + 2)

            act.wait_ge(prod_ready, NG)
            with act.If(wide < WIN):
                for par in range(2):
                    spread_step(par, par, 1)
                with act.Fori(1, NI // 2) as k:
                    for par in range(2):
                        spread_step(2 * k + par, par, k + 1)
                for q in (2, 3):
                    window_out(NI - 1, q)

            k = 0
            for n, (c0, cw) in enumerate(CHUNKS):
                act.wait_ge(s_tail, n + 1)
                act.activation(agg[:, c0:c0 + cw], agg[:, c0:c0 + cw], ACT.Identity, bias=c(C_SU),
                               scale=c(C_S)).then_inc(s_aggm, 1)
                if n >= 1:
                    for h in range(H2):
                        h2_copy(act, k)
                        k += 1
            for h in range(H2):
                h2_copy(act, k)
                k += 1
            act.wait_ge(s_bn2, 2)
            act.activation(colh[:, 8:10], colh[:, 6:8], ACT.Sqrt).then_inc(s_sqrt2, 1)
            act.wait_ge(s_bn2, 6)
            act.activation(h2r[:, 0:N], h2[:, 0:N], ACT.Relu, bias=colh[:, 12:13], scale=colh[:, 10:11]
                           ).then_inc(s_h2r, 1)
            zv = z[0:PN, :].rearrange("p (t f) -> p t f", t=NT)
            zov = zo[0:PN, :].rearrange("p (t f) -> p t f", t=NT)
            m3 = mv3[0:PN, :].rearrange("p (t k) -> p t k", k=2)
            for b, (t0, n) in enumerate(BATCH):
                act.wait_ge(s_zst, b + 1)
                act.activation(rs3[0:PN, t0:t0 + n], m3[:, t0:t0 + n, 1], ACT.Sqrt).then_inc(s_sqrt3, 1)
                if b >= 1:
                    normalise(act, b - 1, zv, zov)
            normalise(act, len(BATCH) - 1, zv, zov)

        @block.vector
        def _(dve):
            chain = [0]

            def link(ins):
                chain[0] += 1
                ins.then_inc(s_dv, 1)
                dve.wait_ge(s_dv, chain[0])

            dve.memset(w1e[:, :, :], 0.0).then_inc(s_w, 1)
            dve.wait_ge(s_rows, 64)
            dve.tensor_copy(srowf[0:NG, :], srow[0:NG, :].bitcast(I32))
            link(dve.tensor_copy(drowf[0:NG, :], drow[0:NG, :].bitcast(I32)))
            dve.tensor_reduce(rowst[0:NG, 0:1], drowf[0:NG, :], AX_X, ALU.min)
            link(dve.tensor_reduce(rowst[0:NG, 1:2], drowf[0:NG, :], AX_X, ALU.max))
            dve.tensor_scalar(drowf[0:NG, :], drowf[0:NG, :], rowst[0:NG, 0:1], None, ALU.subtract).then_inc(s_rowf, 1)
            dve.tensor_tensor(rowst[0:NG, 2:3], rowst[0:NG, 1:2], rowst[0:NG, 0:1], ALU.subtract).then_inc(s_rowf, 1)
            dve.wait_ge(s_cols, 16 * 7)
            link(dve.tensor_scalar(sgn, gbc, 0.0, 2.0, ALU.is_ge, ALU.mult))
            link(dve.tensor_scalar(sgn, sgn, -1.0, None, ALU.add))
            dve.tensor_tensor(w1x[:, :], w1x[:, :], sgn, ALU.mult).then_inc(s_wsgn, 1)
            for a in range(2):
                last = dve.tensor_tensor(w1e[:, a, :], w1e[:, a, :], sgn, ALU.mult)
            last.then_inc(s_wsgn, 1)
            xtv = xt0.rearrange("f (p t) -> f t p", t=NT)
            for b, (t0, n) in enumerate(BATCH):
                dve.wait_ge(s_xps, b + 1)
                dve.tensor_copy(xtv[:, t0:t0 + n, :], psC[b % 2][:, 0:n * PN].rearrange("f (t p) -> f t p", t=n)
                                ).then_inc(s_xt, 1)
            dve.wait_ge(s_rowt, 3)
            dve.tensor_copy(srci[:, :, :].rearrange("p j g -> p (j g)"), psS[:, 0:TILES * NG])
            dve.tensor_copy(loc[:, :, :].rearrange("p j g -> p (j g)"), psX[:, 0:TILES * NG])
            link(dve.tensor_reduce(rowc[0:1, 0:1], psT[1][0:1, 0:NG], AX_X, ALU.max))
            dve.tensor_copy(rowi[0:1, 0:1], rowc[0:1, 0:1])
            link(dve.tensor_copy(basei[0:1, :], psT[0][0:1, 0:NG]))
            dve.memset(col[:, C_M:C_M + 1], 0.0).then_inc(s_idx, 1)

            def onehot_b(i, q):
                g = U * i + q
                if not first(i, q, 4):
                    dve.wait_ge(cnt_ps, g - 3)
                    dve.wait_ge(hot_saved, 16 * i)
                dve.tensor_tensor(hotb[:, q, :].rearrange("p (j w) -> p j w", j=TILES),
                                  iota[:, :].unsqueeze(1).broadcast_to([P, TILES, WIN]),
                                  loc[:, :, bass.ds(g, 1)].broadcast_to([P, TILES, WIN]), ALU.is_equal).then_inc(hotb_ready, 1)

            def add_counts(i, q):
                g = U * i + q
                base = dve.value_load(basei[0:1, bass.ds(g, 1)], min_val=0, max_val=N)
                dve.wait_ge(cnt_ps, g + 1)
                if not first(i, q, 1):
                    dve.wait_ge(cnt_added, g)
                w = cnt[:, bass.ds(base, WIN)]
                dve.tensor_tensor(w, w, psC[q % 2][:, 0:WIN], ALU.add).then_inc(cnt_added, 1)

            def make_h(i, q):
                g = U * i + q
                dve.wait_ge(prod_ready, g + 1)
                dve.wait_ge(gathered[q % 2], 64 * (2 * i + q // 2 + 1))
                if not first(i, q, 2):
                    dve.wait_ge(h_summed, g - 1)
                    dve.wait_ge(sq_ready, g - 1)
                    if q == 1:
                        dve.wait_ge(spilled, 16 * i)
                    else:
                        dve.wait_ge(kept, {0: 3 * i, 2: 3 * i + 1, 3: 3 * i + 2}[q])
                dve.tensor_tensor(hs[:, q % 2, :], psH[q % 2][:, :], yg[:, q % 2, :], ALU.add).then_inc(h_ready, 1)

            def sum_h(i, q):
                g = U * i + q
                dve.wait_ge(h_ready, g + 1)
                if not first(i, q, 1):
                    dve.wait_ge(h_summed, g)
                dve.tensor_tensor(psS[:, :], hs[:, q % 2, :], psS[:, :], ALU.add).then_inc(h_summed, 1)

            def sum_sq(i, q):
                g = U * i + q
                dve.wait_ge(sq_ready, g + 1)
                if not first(i, q, 1):
                    dve.wait_ge(sq_summed, g)
                dve.tensor_tensor(psX[:, :], sq[:, q % 2, :], psX[:, :], ALU.add).then_inc(sq_summed, 1)

            def stage_idx(i, q):
                dve.tensor_copy(idx[:, q, :].unsqueeze(2), srci[:, :, bass.ds(U * i + q, 1)]).then_inc(idx_staged, 1)

            def edge_step(i):
                for q in range(U):
                    make_h(i, q)
                    if not (isinstance(i, int) and i == NI - 1):
                        stage_idx(i + 1, q)
                    if q < U - 1:
                        onehot_b(i, q + 1)
                    elif not (isinstance(i, int) and i == NI - 1):
                        onehot_b(i + 1, 0)
                    sum_h(i, q)
                    add_counts(i, q)
                    sum_sq(i, q)

            dve.wait_ge(s_set, 1)
            dve.wait_ge(s_idx, 1)
            link(dve.tensor_scalar(c(C_AG), c(C_G), 0.0, 2.0, ALU.is_ge, ALU.mult))
            link(dve.tensor_scalar(c(C_AG), c(C_AG), -1.0, None, ALU.add))
            link(dve.tensor_tensor(c(C_B1), c(C_B1), c(C_AG), ALU.mult))
            link(dve.tensor_tensor(c(C_AG), c(C_G), c(C_AG), ALU.mult))
            for q in range(U):
                stage_idx(0, q)
            onehot_b(0, 0)
            dve.memset(psS[:, :], 0.0)
            dve.memset(psX[:, :], 0.0)
            edge_step(0)
            with dve.Fori(1, NI - 1) as i:
                edge_step(i)
            edge_step(NI - 1)

            dve.wait_ge(sq_summed, NG)
            dve.tensor_reduce(sq[:, 0, 0:F], psS[:, :].rearrange("p (j f) -> p f j", j=TILES), AX_X, ALU.add)
            dve.tensor_reduce(sq[:, 0, F:2 * F], psX[:, :].rearrange("p (j f) -> p f j", j=TILES), AX_X, ALU.add
                              ).then_inc(s_folded, 1)
            dve.wait_ge(cnt_added, NG)
            link(dve.tensor_scalar(agg[:, :], cnt[:, :], 0.0, None, ALU.is_equal))

            def bn(ins):
                bnc[0] += 1
                ins.then_inc(s_bn1, 1)
                dve.wait_ge(s_bn1, bnc[0])

            bnc = [0]
            dve.wait_ge(s_folded, 2)
            bn(dve.tensor_scalar(c(C_M, 2), psT[0][:, 0:2], 1.0 / E, None, ALU.mult))
            bn(dve.tensor_tensor(c(C_V), c(C_M), c(C_M), ALU.mult))
            bn(dve.tensor_tensor(c(C_V), c(C_Q), c(C_V), ALU.subtract))
            bn(dve.tensor_scalar(c(C_V), c(C_V), 0.0, EPS, ALU.max, ALU.add))
            bn(dve.tensor_tensor(c(C_M), c(C_M), c(C_B1), ALU.add))
            bn(dve.tensor_tensor(c(C_M), c(C_B1), c(C_M), ALU.subtract))
            dve.wait_ge(s_sqrt1, 1)
            bn(dve.reciprocal(c(C_R), c(C_SD)))
            bn(dve.tensor_scalar(c(C_S), c(C_R), c(C_AG), TINY, ALU.mult, ALU.max))
            bn(dve.reciprocal(c(C_T), c(C_S)))
            bn(dve.scalar_tensor_tensor(out=c(C_U), in0=c(C_T), scalar=c(C_BE), in1=c(C_M), op0=ALU.mult,
                                        op1=ALU.add))
            dve.tensor_tensor(c(C_SU), c(C_S), c(C_U), ALU.mult)
            dve.wait_ge(spilled, 16 * NI)
            dve.memset(work[:, 3, F:2 * F], 1.0)
            dve.tensor_scalar(work[:, 3, 0:F], ident[:, :], c(C_U), -1.0, ALU.mult, ALU.mult).then_inc(s_uin, 1)
            dve.tensor_scalar(agg[:, :], agg[:, :], c(C_U), -1.0, ALU.mult, ALU.mult).then_inc(agg_set, 1)
            dve.wait_ge(agg_set, 1)
            dve.wait_ge(s_ups, 1)

            def maxes(i, q):
                g = U * i + q
                if not first(i, q, 4):
                    dve.wait_ge(summed, g - 3)
                if q < KEEP:
                    hin = resg(i, q)
                else:
                    dve.wait_ge(reload, 16 * (i + 1))
                    hin = back if isinstance(i, int) and i == 0 else resg(i - 1, 0)
                dve.tensor_tensor(mx[:, q, :], hin, negu, ALU.max).then_inc(m_ready, 1)

            def sum_step(i):
                for q in range(U):
                    maxes(i, q)

            dve.wait_ge(kept, NI * KEEP)
            wide = dve.value_load(rowi[0:1, 0:1], min_val=0, max_val=N)
            with dve.If(wide < WIN):
                dve.sem_inc(s_masked, 1)
                sum_step(0)
                invert_counts(dve)
                with dve.Fori(1, NI) as i:
                    sum_step(i)
            with dve.Else():
                general(dve, resg)
            dve.wait_ge(sums_over, 1)
            dve.wait_ge(s_rcb, 16)

            bsv = bs2.rearrange("p (h n s) -> p h n s", h=H2, s=6)

            def mean(n):
                c0, cw = CHUNKS[n]
                dve.tensor_tensor(agg[:, c0:c0 + cw], agg[:, c0:c0 + cw], cnt[:, c0:c0 + cw], ALU.mult
                                  ).then_inc(s_tail, 1)

            for n in range(2):
                mean(n)
            for k in range(NC * H2):
                n, h = k // H2, k % H2
                if h == 0 and n + 2 < NC:
                    mean(n + 2)
                c0, cw = CHUNKS[n]
                dve.wait_ge(s_h2, k + 1)
                ins = dve.bn_stats(bsv[:, h, n, :], h2[:, h * N + c0:h * N + c0 + cw])
                ins.then_inc(s_h2st, 1)
            dve.wait_ge(s_h2st, NC * H2)
            for h in range(H2):
                last = dve.bn_aggr(mv2[:, 2 * h:2 * h + 2], bsv[:, h, :, :].rearrange("p n s -> p (n s)"))
            bn2 = [0]

            def b2n(ins):
                bn2[0] += 1
                ins.then_inc(s_bn2, 1)
                dve.wait_ge(s_bn2, bn2[0])

            dve.wait_ge(s_nodein, 16 * 11)
            mvv = mv2.rearrange("p (h k) -> p h k", k=2)
            b2n(last)
            b2n(dve.tensor_scalar(colh[:, 6:8], mvv[:, :, 1], EPS, None, ALU.add))
            b2n(dve.tensor_tensor(colh[:, 14:16], mvv[:, :, 0], colh[:, 4:6], ALU.add))
            dve.wait_ge(s_sqrt2, 1)
            b2n(dve.reciprocal(colh[:, 10:12], colh[:, 8:10]))
            link(dve.tensor_tensor(colh[:, 10:12], colh[:, 10:12], colh[:, 0:2], ALU.mult))
            link(dve.tensor_tensor(colh[:, 14:16], colh[:, 4:6], colh[:, 14:16], ALU.subtract))
            b2n(dve.tensor_tensor(colh[:, 12:14], colh[:, 14:16], colh[:, 10:12], ALU.mult))
            b2n(dve.tensor_tensor(colh[:, 12:14], colh[:, 12:14], colh[:, 2:4], ALU.add))
            dve.wait_ge(s_h2, NC * H2)
            link(dve.tensor_scalar(h2[:, N:2 * N], h2[:, N:2 * N], colh[:, 11:12], colh[:, 13:14], ALU.mult, ALU.add))
            dve.tensor_scalar(h2r[:, N:2 * N], h2[:, N:2 * N], 0.0, None, ALU.max).then_inc(s_h2r, 1)
            zv = z[0:PN, :].rearrange("p (t f) -> p t f", t=NT)
            b3 = bs3[0:PN, :].rearrange("p (t s) -> p t s", s=6)
            m3 = mv3[0:PN, :].rearrange("p (t s) -> p t s", s=2)

            def scales(b):
                t0, n = BATCH[b]
                dve.wait_ge(s_sqrt3, b + 1)
                r = rs3[0:PN, t0:t0 + n]
                link(dve.reciprocal(r, r))
                dve.scalar_tensor_tensor(out=nm3[0:PN, t0:t0 + n], in0=m3[:, t0:t0 + n, 0], scalar=-1.0, in1=r,
                                         op0=ALU.mult, op1=ALU.mult).then_inc(s_ln, 1)

            for b, (t0, n) in enumerate(BATCH):
                dve.wait_ge(s_ops, b + 1)
                zb = z[0:PN, t0 * F:(t0 + n) * F]
                o = BANK[b % 4][0:PN, 0:n * F]
                ov = o.rearrange("p (t f) -> p t f", t=n)
                dve.tensor_tensor(ov, ov, blr[0:PN, :].unsqueeze(1).broadcast_to([PN, n, F]), ALU.add
                                  ).then_inc(s_bl, 1)
                dve.wait_ge(s_bl, b + 1)
                dve.scalar_tensor_tensor(out=zb, in0=o, scalar=0.0,
                                         in1=xn[0:PN, t0 * F:(t0 + n) * F], op0=ALU.max, op1=ALU.add
                                         ).then_inc(s_z, 1)
                dve.wait_ge(s_z, b + 1)
                for t in range(t0, t0 + n):
                    ins = dve.bn_stats(b3[:, t, :], zv[:, t, :])
                link(ins)
                for t in range(t0, t0 + n):
                    ins = dve.bn_aggr(m3[:, t, :], b3[:, t, :])
                link(ins)
                dve.tensor_scalar(m3[:, t0:t0 + n, 1], m3[:, t0:t0 + n, 1], EPS, None, ALU.add).then_inc(s_zst, 1)
                if b >= 1:
                    scales(b - 1)
            scales(len(BATCH) - 1)


_INS = ['x', 'src', 'dst', 'edge_attr_64', 'L0_gnn_W1', 'L0_gnn_b1', 'L0_gnn_g1', 'L0_gnn_be1', 'L0_gnn_W2',
        'L0_gnn_b2', 'L0_gnn_g2', 'L0_gnn_be2', 'L0_gnn_Wl', 'L0_gnn_bl']


def kernel(**inputs):
    import numpy as np
    import concourse.bacc as bacc
    from concourse.bass_utils import run_bass_kernel_spmd as run

    nc = bacc.Bacc("TRN2", target_bir_lowering=False, num_devices=1)
    arrays, args = {}, []
    for name in _INS:
        a = np.ascontiguousarray(inputs[name])
        arrays[f"in_{name}"] = a
        args.append(nc.dram_tensor(f"in_{name}", a.shape, mybir.dt.from_np(a.dtype), kind="ExternalInput").ap())
    shape = inputs['x'].shape
    args.append(nc.dram_tensor("out_dram", shape, F32, kind="ExternalOutput").ap())
    gnn_kernel(nc, *args)
    r = run(nc, [arrays], core_ids=[0])
    return r.results[0]["out_dram"]
```

```python
from contextlib import ExitStack

import concourse.bass as bass
from concourse import mybir

F32 = mybir.dt.float32
BF16 = mybir.dt.bfloat16
I32 = mybir.dt.int32
ALU = mybir.AluOpType
ACT = mybir.ActivationFunctionType
AX_X = mybir.AxisListType.X

P = 128
EPS = 1e-5
TINY = 1e-20
TILES = 4
GROUP = TILES * P
U = 4
KEEP = 3
WIN = 64
BEYOND = 64
WIDE = 256


def gnn_kernel(nc, x, src, dst, ea, W1, b1, g1, be1, W2, b2, g2, be2, Wl, bl, out):
    N, F = x.shape
    E, FE = ea.shape
    H2 = W2.shape[1] // P
    NT = 25
    PN = N // NT
    NG = (E + GROUP - 1) // GROUP
    NI = NG // U
    assert F == P and FE * 2 == P and NT * PN == N and NG == NI * U and H2 == 2
    LAST = E - (NG - 1) * GROUP
    LP = LAST // TILES
    LR = LAST - LP * TILES
    PAD = N
    YROWS = 25 * P
    NB = (N + WIDE) // WIDE
    NAGG = NB * WIDE
    assert NAGG >= N + WIN and NI % 2 == 0
    CH = 4 * PN
    CHUNKS = [(c, min(CH, N - c)) for c in range(0, N, CH)]
    NC = len(CHUNKS)
    DVE_MEAN = 2
    DVE_RELU = 6
    BATCH = [(t, min(4, NT - t)) for t in range(0, NT, 4)]
    DVE_NORM = [int(3 <= b < len(BATCH) - 1) for b in range(len(BATCH))]
    POOL_Z = list(range(1, len(BATCH) - 1))
    XLOADS = [BATCH[0:1], BATCH[1:2], BATCH[2:4], BATCH[4:]]
    YSAVES = [BATCH[0:2], BATCH[2:4], BATCH[4:6], BATCH[6:]]

    ytab = nc.dram_tensor("ytab", (YROWS, F), F32, kind="Internal").ap()
    h2x_dram = nc.dram_tensor("h2x_dram", (NT, P, H2 * PN), F32, kind="Internal").ap()
    spill = nc.dram_tensor("spill", (NI, P, TILES * F), F32, kind="Internal").ap()
    rc_dram = nc.dram_tensor("rc_dram", (N,), F32, kind="Internal").ap()
    hot_dram = nc.dram_tensor("hot_dram", (NI, P, U * TILES * WIN), BF16, kind="Internal").ap()

    ctx = ExitStack()
    with ctx:
        def sb(name, shape, dt=F32):
            return ctx.enter_context(nc.sbuf_tensor(name, shape, dt))

        def pb(name, shape):
            return ctx.enter_context(nc.psum_tensor(name, shape, F32))

        def sem(name):
            return ctx.enter_context(nc.semaphore(name))

        GF = TILES * F
        res = sb("res", [P, NI * KEEP * GF])
        work = sb("work", [P, 6, GF])
        yg = work[:, 0:2, :]
        hs = work[:, 2:4, :]
        sq = work[:, 4:6, :]
        mx = work[:, 0:4, :]
        back = work[:, 4, :]
        work2 = sb("work2", [P, 4, TILES * WIN])
        ear = work2[:, 0:2, :]
        eat = work2[:, 2:4, :]
        hotf = work2
        hotb = sb("hotb", [P, U, TILES * WIN], BF16)
        hotb2 = work[:, 5, :].bitcast(BF16).rearrange("p (q w) -> p q w", q=U)
        agg = sb("agg", [P, NAGG])
        cnt = sb("cnt", [P, NAGG])
        srci = sb("srci", [P, TILES, NG], I32)
        idx = sb("idx", [P, U, TILES], I32)
        loc = sb("loc", [P, TILES, NG])
        basei = sb("basei", [1, NG], I32)
        ident = sb("ident", [P, P])
        w1x = sb("w1x", [P, F])
        w1e = sb("w1e", [P, 2, F])
        iota = sb("iota", [P, WIN])
        ones = sb("ones", [P, 1])
        onesb = sb("onesb", [P, P], BF16)
        epsc = sb("epsc", [P, 1])
        col = sb("col", [P, 24])
        cntc = sb("cntc", [P, NT])
        rowc = sb("rowc", [1, 4])
        rowi = sb("rowi", [1, 4], I32)

        RCN = NI // 2 - 5
        RCP = (N - 1) // RCN // 8 * 8
        XTP = NT // RCN
        NODEIN = 16 * ((H2 + 1) * (RCN + 1) + 3 + 3 * H2)
        TAB = 16 * (len(YSAVES) + 1)
        ghot = work2[:, :, :].rearrange("p q w -> p (q w)")
        wsum = srci[:, :, :].rearrange("p j g -> p (j g)").bitcast(F32)[:, 0:U * WIN].rearrange(
            "p (q w) -> p q w", q=U)
        giota = hotb[:, :, :].rearrange("p q w -> p (q w)").bitcast(F32)

        at = NI * KEEP * GF

        def tail(n):
            nonlocal at
            at -= n
            return res[:, at:at + n]

        xt0 = tail(N)
        xn0 = tail(NT * F)
        ysb = tail(NT * F)
        srow = tail(GROUP)
        drow = tail(GROUP)
        srowf = tail(GROUP)
        drowf = tail(GROUP)
        rowst = tail(4)
        zeros = tail(F)
        sgn = tail(F)
        gbc = tail(F)

        near = 0

        def head(n):
            nonlocal near
            near += n
            return res[:, near - n:near]

        h2 = head(H2 * N)
        xn = head(NT * F)
        w2 = head(H2 * P)
        wl = head(H2 * F)
        blr = head(F)
        nbl = head(F)
        zo = head(NT * F)
        h2r = head(H2 * N)
        z = head(NT * F)
        bs2 = head(NC * 6)
        sm2 = head(2 * NC)
        junk = head(4 * CH)
        bs3 = head(NT * 6)
        mv3 = head(NT * 2)
        rs3 = head(NT)
        nm3 = head(NT)
        colh = head(16)
        mv2 = head(2 * H2)

        assert H2 * N + NT * F + (H2 + H2 + 1) * P <= 9 * KEEP * GF and near <= (NI - 3) * KEEP * GF

        w2x = agg[:, 0:H2 * P]
        h2x = agg[:, H2 * P:H2 * P + H2 * PN]
        assert NT == NI - 1 and all((i + 1) * KEEP * GF <= NI * KEEP * GF - N + i * PN for i in range(NT))

        psT = [pb(f"psT{i}", [P, 512]) for i in range(2)]
        psH = [pb(f"psH{i}", [P, GF]) for i in range(2)]
        psC = [pb(f"psC{i}", [P, GF]) for i in range(2)]
        psS = pb("psS", [P, 512])
        psX = pb("psX", [P, 512])
        psA = [psH[0], psH[1], psC[0], psC[1]]

        negu = psX[:, 0:F].unsqueeze(1).broadcast_to([P, TILES, F])
        BANK = [psT[0], psT[1], psS] + psA

        s_x = [sem(f"x_loaded{k}") for k in range(len(XLOADS))]
        s_w1x = sem("w1x_loaded")
        s_w = sem("w_loaded")
        s_rowset = sem("rows_preset")
        s_rows = sem("rows_loaded")
        s_cols = sem("cols_loaded")
        s_ident = sem("ident_ready")
        s_pool = sem("pool_chain")
        s_wsgn = sem("w1_signed")
        s_dv = sem("dve_chain")
        s_rowf = sem("rows_as_float")
        s_rowt = sem("rows_turned")
        s_idx = sem("indices_ready")
        s_xps = sem("x_turned_psum")
        s_xt = sem("xt_ready")
        s_yps = sem("y_psum")
        s_ysb = sem("y_ready")
        s_zr = sem("zeros_ready")
        s_tab = sem("table_written")
        x_ps = sem("w2_x_psum")
        x_out = sem("w2_x_copied")
        x_saved = sem("w2_x_saved")
        ea_loaded = [sem(f"ea_loaded{i}") for i in range(2)]
        ea_turned = sem("ea_turned")
        eat_ready = sem("eat_ready")
        prod_ready = sem("ea_product_ready")
        idx_staged = sem("idx_staged")
        gathered = [sem(f"gathered{i}") for i in range(2)]
        h_ready = sem("h_ready")
        sq_ready = sem("sq_ready")
        h_summed = sem("h_summed")
        sq_summed = sem("sq_summed")
        s_folded = sem("sums_folded")
        kept = sem("kept")
        spilled = sem("spilled")
        hotb_ready = sem("hotb_ready")
        cnt_ps = sem("cnt_psum_ready")
        cnt_added = sem("cnt_added")
        s_set = sem("memory_preset")
        s_bn1 = sem("bn1_chain")
        s_sqrt1 = sem("bn1_sqrt")
        s_uin = sem("diag_u_ready")
        s_ups = sem("u_spread")
        reload = sem("group_back")
        slot_passed = sem("slot_passed")
        hot_saved = sem("hot_saved")
        hot_back = [sem(f"hot_back{i}") for i in range(2)]
        sums_over = sem("sums_over")
        s_masked = sem("edgeless_marked")
        s_cc = sem("counts_compact")
        s_rc = sem("reciprocals_ready")
        s_rcd = sem("reciprocals_in_dram")
        s_rcb = sem("reciprocals_spread")
        g_base = sem("general_base_spread")
        g_back = sem("general_group_back")
        g_m = sem("general_max_ready")
        g_iota = sem("general_iota_ready")
        g_hot = sem("general_hot_ready")
        g_summed = sem("general_summed")
        g_added = sem("general_added")
        hotf_ready = sem("hotf_ready")
        m_ready = sem("max_ready")
        summed = sem("window_summed")
        agg_set = sem("agg_preset")
        wsum_ready = sem("window_copied")
        agg_added = sem("agg_added")
        s_nodein = sem("node_inputs_loaded")
        s_mean = sem("mean_ready")
        s_meanp = sem("mean_ready_gpsimd")
        s_w2s = sem("w2_scaled")
        s_sm2 = sem("h2_sums")
        s_h2ps = sem("h2_psum")
        s_h2 = sem("h2_copied")
        s_h2st = sem("h2_stats")
        s_bn2 = sem("bn2_chain")
        s_sqrt2 = sem("bn2_sqrt")
        s_h2n = sem("h2_normalised")
        s_h2r = sem("h2_relu")
        s_h2rd = sem("h2_relu_dve")
        s_ops = sem("out_psum")
        s_relu = sem("out_relu")
        s_z = sem("z_ready")
        s_zd = sem("z_ready_dve")
        s_sqrt3 = sem("ln_sqrt")
        s_ln = sem("ln_scale_ready")
        s_bl = sem("bl_in_x")
        s_rst = sem("row_stats")
        s_rag = sem("row_stats_joined")
        s_rs = sem("row_rstd")
        s_zo = sem("out_rows_ready")
        s_zod = sem("out_rows_ready_dve")
        s_out = sem("out_written")

        C_SUM, C_G, C_BE, C_B1, C_M, C_Q, C_V, C_SD, C_R, C_S, C_T, C_U, C_AG = range(13)

        k2 = col[:, 14:20]

        def c(i, n=1):
            return col[:, i:i + n]

        def resg(i, q):
            return res[:, bass.ds((i * KEEP + q) * GF, GF)]

        def sq_fold(k):
            return sq[:, 0, k * F:(k + 1) * F]

        def tiles(g):
            return g.rearrange("p (j f) -> p j f", j=TILES)

        def first(i, q, back_by):
            return isinstance(i, int) and U * i + q < back_by

        def normalise(act, b, zv, zov):
            t0, n = BATCH[b]
            act.wait_ge(s_ln, b + 1)
            for t in range(t0, t0 + n - DVE_NORM[b]):
                act.activation(zov[:, t, :], zv[:, t, :], ACT.Identity, bias=nm3[0:PN, t:t + 1],
                               scale=rs3[0:PN, t:t + 1]).then_inc(s_zo, 1)

        def counts_out(q):
            q.dma_start(cntc[0:PN, :], cnt[0:1, 0:N]).then_inc(s_cc, 16)

        def counts_to_dram(q):
            q.wait_ge(s_rc, 2)
            q.dma_start(rc_dram.rearrange("(p t) -> p t", t=NT), cntc[0:PN, :]).then_inc(s_rcd, 16)

        def counts_back(q, k):
            q.dma_start(cnt[:, bass.ds(k * RCP, RCP)], rc_dram[bass.ds(k * RCP, RCP)].partition_broadcast(P)
                        ).then_inc(s_rcb, 16)

        def last_counts_back(q):
            q.dma_start(cnt[:, RCN * RCP:N], rc_dram[RCN * RCP:N].partition_broadcast(P)).then_inc(s_rcb, 16)

        def invert_counts(dve):
            dve.wait_ge(s_cc, 16)
            dve.tensor_scalar(cntc[0:PN, :], cntc[0:PN, :], 1.0, None, ALU.max).then_inc(s_rc, 1)
            dve.wait_ge(s_rc, 1)
            dve.reciprocal(cntc[0:PN, :], cntc[0:PN, :]).then_inc(s_rc, 1)

        def general(dve, resg):
            iota0, now = giota[:, 0:WIDE], giota[:, WIDE:2 * WIDE]
            dve.tensor_copy(work[0:1, 2, 0:NG], basei[0:1, :]).then_inc(g_base, 1)
            dve.wait_ge(agg_set, 3)
            dve.memset(agg[:, :], 0.0)
            dve.memset(cnt[:, :], 0.0)
            dve.wait_ge(hot_saved, 16 * NI)
            for k in range(WIDE // WIN):
                dve.tensor_scalar(giota[:, k * WIN:(k + 1) * WIN], iota[:, :], float(k * WIN), None, ALU.add)
            dve.wait_ge(g_base, 2)
            dve.tensor_tensor(loc[:, :, :], loc[:, :, :],
                              psT[0][:, 0:NG].unsqueeze(1).broadcast_to([P, TILES, NG]), ALU.add).then_inc(g_iota, 1)
            with dve.Fori(0, NI) as i:
                for q in range(U):
                    g = U * i + q
                    if q == KEEP:
                        dve.wait_ge(g_back, 16 * (i + 1))
                    dve.tensor_tensor(tiles(mx[:, 0, :]), tiles(resg(i, q) if q < KEEP else back), negu, ALU.max
                                      ).then_inc(g_m, 1)
                    dve.wait_ge(g_iota, (NB + 1) * g + 1)
                    dve.tensor_copy(now, iota0).then_inc(g_iota, 1)
                    with dve.Fori(0, NB) as b:
                        dve.wait_ge(g_iota, (NB + 1) * g + b + 2)
                        for j in range(TILES):
                            last = dve.tensor_scalar(ghot[:, j * WIDE:(j + 1) * WIDE], now,
                                                     loc[:, j, bass.ds(g, 1)], None, ALU.is_equal)
                        last.then_inc(g_hot, 1)
                        dve.wait_ge(g_hot, NB * g + b + 1)
                        dve.tensor_scalar(now, now, float(WIDE), None, ALU.add).then_inc(g_iota, 1)
                        dve.wait_ge(g_summed, NB * g + b + 1)
                        a = agg[:, bass.ds(b * WIDE, WIDE)]
                        n = cnt[:, bass.ds(b * WIDE, WIDE)]
                        dve.tensor_tensor(a, a, psH[0][:, 0:WIDE], ALU.add)
                        dve.tensor_tensor(n, n, psH[1][:, 0:WIDE], ALU.add).then_inc(g_added, 1)
                        dve.wait_ge(g_added, NB * g + b + 1)
            none = res[:, NI * KEEP * GF - NAGG:NI * KEEP * GF]
            dve.tensor_scalar(none, cnt[:, :], 0.0, None, ALU.is_equal).then_inc(g_added, 1)
            dve.wait_ge(g_added, NB * NG + 1)
            dve.sem_inc(s_masked, 1)
            dve.tensor_scalar(none, none, c(C_U), -1.0, ALU.mult, ALU.mult).then_inc(g_added, 1)
            dve.wait_ge(g_added, NB * NG + 2)
            dve.tensor_tensor(agg[:, :], agg[:, :], none, ALU.add)
            invert_counts(dve)
            dve.drain().then_inc(sums_over, 1)

        block = ctx.enter_context(nc.Block())

        @block.sync
        def _(sp):
            def load_lists():
                sp.wait_ge(s_rowset, 1)
                for r, d in ((srow, src), (drow, dst)):
                    sp.dma_start(r[0:NG - 1, :].bitcast(I32),
                                  d[0:(NG - 1) * GROUP].rearrange("(g e) -> g e", e=GROUP)).then_inc(s_rows, 16)
                    sp.dma_start(r[NG - 1:NG, 0:LAST].bitcast(I32),
                                  d[(NG - 1) * GROUP:E].rearrange("(g e) -> g e", g=1)).then_inc(s_rows, 16)

            xv = x.rearrange("(p t) f -> p t f", t=NT)
            xnv = xn0[0:PN, :].rearrange("p (t f) -> p t f", t=NT)
            for k, part in enumerate(XLOADS):
                t, n = part[0][0], sum(w for _, w in part)
                if k == 2:
                    load_lists()
                sp.dma_start(xnv[:, t:t + n, :], xv[:, t:t + n, :]).then_inc(s_x[k], 16)
            sp.wait_ge(s_w, 1)
            sp.dma_start(w1e[0:FE, 0, :], W1[F:F + FE, :]).then_inc(s_cols, 16)
            sp.dma_start(w1e[FE:P, 1, :], W1[F:F + FE, :]).then_inc(s_cols, 16)
            sp.dma_start(w2x, W2[0:F, :]).then_inc(s_cols, 16)
            for k, v in ((C_G, g1), (C_BE, be1), (C_B1, b1)):
                sp.dma_start(c(k), v.rearrange("(p a) -> p a", a=1)).then_inc(s_cols, 16)
            sp.wait_ge(s_zr, 1)
            sp.dma_start(ytab[N:YROWS, :], zeros[0:YROWS - N, :]).then_inc(s_tab, 16)
            yv = ytab[0:N, :].rearrange("(p t) f -> p t f", t=NT)
            ysv = ysb[0:PN, :].rearrange("p (t f) -> p t f", t=NT)
            done = 0
            for part in YSAVES:
                t, n = part[0][0], sum(w for _, w in part)
                done += len(part)
                sp.wait_ge(s_ysb, done)
                sp.dma_start(yv[:, t:t + n, :], ysv[:, t:t + n, :]).then_inc(s_tab, 16)

            def load_ea(i, q):
                if not first(i, q, 2):
                    sp.wait_ge(ea_turned, U * i + q - 1)
                s = ea_loaded[q % 2]
                sp.dma_start(ear[:, q % 2, :],
                             ea[bass.ds((i * U + q) * GROUP, GROUP), :].rearrange(
                                 "(p j) f -> p (j f)", j=TILES)).then_inc(s, 16)

            for q in range(U):
                load_ea(0, q)
            for k, v in enumerate((g2, be2, b2)):
                for h in range(H2):
                    sp.dma_start(k2[:, 2 * k + h:2 * k + h + 1],
                                 v[h * P:(h + 1) * P].rearrange("(p a) -> p a", a=1)).then_inc(s_nodein, 16)
            with sp.Fori(1, NI - 1) as i:
                for q in range(U):
                    load_ea(i, q)
            for q in range(U - 1):
                load_ea(NI - 1, q)
            sp.wait_ge(ea_turned, NG - 2)
            sp.wait_ge(s_tab, TAB)
            e0 = (NG - 1) * GROUP
            s = ea_loaded[1]
            sp.dma_start(ear[0:LP, 1, :],
                         ea[e0:e0 + LP * TILES, :].rearrange("(p j) f -> p (j f)", j=TILES)).then_inc(s, 16)
            sp.dma_start(ear[LP:LP + 1, 1, 0:LR * FE],
                         ea[e0 + LP * TILES:E, :].rearrange("(p j) f -> p (j f)", p=1)).then_inc(s, 16)
            zr = ytab[N:YROWS, :].rearrange("r f -> (r f)")
            n1 = (TILES - LR) * FE
            sp.dma_start(ear[LP:LP + 1, 1, LR * FE:],
                         zr[0:n1].rearrange("(p f) -> p f", p=1)).then_inc(s, 16)
            n2 = (P - LP - 1) * TILES * FE
            sp.dma_start(ear[LP + 1:P, 1, :],
                         zr[n1:n1 + n2].rearrange("(p f) -> p f", f=TILES * FE)).then_inc(s, 16)

            sp.wait_ge(spilled, 16 * NI)
            sp.wait_ge(hot_saved, 16 * NI)
            sp.wait_ge(s_folded, 3)
            wide = sp.value_load(rowi[0:1, 0:1], min_val=0, max_val=N)

            def load_hot(i, par):
                sp.dma_start((hotb, hotb2)[par][:, :, :].rearrange("p q w -> p (q w)"),
                             hot_dram[bass.ds(i, 1), :, :].rearrange("a p w -> (a p) w")
                             ).then_inc(hot_back[par], 16)

            def load_back(i):
                sp.wait_ge(m_ready, U * i + 1)
                sp.sem_inc(slot_passed, 1)
                sp.wait_ge(reload, 16 * (i + 1))
                sp.sem_inc(slot_passed, 1)
                sp.dma_start(resg(i, 0), spill[bass.ds(i + 1, 1), :, :].rearrange("a p f -> (a p) f")
                             ).then_inc(reload, 16)

            h2v = h2.rearrange("p (h t c) -> p h t c", h=H2, t=NT)
            xnv2 = xn[0:PN, :].rearrange("p (t f) -> p t f", t=NT)

            def load_nodes(k, half):
                for h in range(H2 if half == 0 else 0):
                    sp.dma_start(h2v[:, h, bass.ds(k * XTP, XTP), :],
                                 h2x_dram[bass.ds(k * XTP, XTP), :, h * PN:(h + 1) * PN].rearrange("t p c -> p t c")
                                 ).then_inc(s_nodein, 16)
                if half == 1:
                    sp.dma_start(xnv2[:, bass.ds(k * XTP, XTP), :],
                                 x[bass.ds(k * XTP * PN, XTP * PN), :].rearrange("(t p) f -> p t f", p=PN)
                                 ).then_inc(s_nodein, 16)
                    counts_back(sp, k)

            def load_rest():
                last_counts_back(sp)
                for h in range(H2):
                    sp.dma_start(h2v[:, h, RCN * XTP:NT, :],
                                 h2x_dram[RCN * XTP:NT, :, h * PN:(h + 1) * PN].rearrange("t p c -> p t c")
                                 ).then_inc(s_nodein, 16)
                sp.dma_start(xnv2[:, RCN * XTP:NT, :],
                             x[RCN * XTP * PN:N, :].rearrange("(t p) f -> p t f", p=PN)).then_inc(s_nodein, 16)

            def load_weights():
                sp.dma_start(w2, W2[F:2 * F, :]).then_inc(s_nodein, 16)
                sp.dma_start(wl.rearrange("p (k c) -> p k c", k=H2), Wl.rearrange("(k p) c -> p k c", k=H2)
                             ).then_inc(s_nodein, 16)
                sp.dma_start(blr[0:PN, :], bl.partition_broadcast(PN)).then_inc(s_nodein, 16)

            with sp.If(wide < WIN):
                load_hot(0, 0)
                sp.dma_start(back, spill[0, :, :]).then_inc(reload, 16)
                load_hot(1, 1)
                load_back(0)
                sp.wait_ge(agg_set, 2)
                counts_out(sp)

                def load_step(i, par):
                    sp.wait_ge(hotf_ready, U * (i - 1))
                    sp.sem_inc(slot_passed, 1)
                    load_hot(i, par)
                    load_back(i - 1)

                load_step(2, 0)
                counts_to_dram(sp)
                load_step(3, 1)
                sp.wait_ge(s_rcd, 16)
                with sp.Fori(2, 5) as k:
                    for par in range(2):
                        load_step(2 * k + par, par)
                load_weights()
                with sp.Fori(5, NI // 2) as k:
                    for par in range(2):
                        load_step(2 * k + par, par)
                        load_nodes(k - 5, par)
                load_rest()
            with sp.Else():
                sp.dma_start(back, spill[0, :, :]).then_inc(g_back, 16)
                with sp.Fori(1, NI) as i:
                    sp.wait_ge(g_m, U * i)
                    sp.sem_inc(slot_passed, 1)
                    sp.dma_start(back, spill[bass.ds(i, 1), :, :].rearrange("a p f -> (a p) f")
                                 ).then_inc(g_back, 16)
                sp.wait_ge(g_m, NG)
                sp.wait_ge(s_masked, 1)
                counts_out(sp)
                counts_to_dram(sp)
                sp.wait_ge(s_rcd, 16)
                with sp.Fori(0, RCN) as k:
                    for half in range(2):
                        load_nodes(k, half)
                load_weights()
                load_rest()
            ov = out.rearrange("(t p) f -> p t f", p=PN)
            zov = zo[0:PN, :].rearrange("p (t f) -> p t f", t=NT)
            for b, (t, n) in enumerate(BATCH):
                by_dve = sum(DVE_NORM[:b + 1])
                sp.wait_ge(s_zo, t + n - by_dve)
                if by_dve:
                    sp.wait_ge(s_zod, by_dve)
                sp.dma_start(ov[:, t:t + n, :], zov[:, t:t + n, :]).then_inc(s_out, 16)
            sp.wait_ge(s_out, 16 * len(BATCH))

        @block.gpsimd
        def _(pool):
            pool.memset(srow.bitcast(I32), PAD)
            pool.memset(drow.bitcast(I32), PAD).then_inc(s_rowset, 1)
            pool.memset(ident[:, :], 0.0).then_inc(s_pool, 1)
            pool.wait_ge(s_pool, 1)
            pool.affine_select(out=ident[:, :], in_=ident[:, :], compare_op=ALU.not_equal, fill=1.0, base=0,
                               pattern=[[-1, P]], channel_multiplier=1).then_inc(s_ident, 1)
            pool.memset(zeros, 0.0).then_inc(s_zr, 1)
            pool.iota(iota[:, :], [[1, WIN]], base=0, channel_multiplier=0,
                      allow_small_or_imprecise_dtypes=True)
            pool.memset(onesb[:, :], 1.0)
            pool.memset(ones[:, :], 1.0)
            pool.memset(epsc[:, :], EPS)
            pool.memset(cnt[:, :], 0.0)
            pool.drain().then_inc(s_set, 1)
            pool.wait_ge(s_tab, TAB)

            def gather(i, q):
                if not first(i, q, 2):
                    pool.wait_ge(h_ready, U * i + q - 1)
                pool.wait_ge(idx_staged, U * i + q + 1)
                pool.sem_inc(slot_passed, 1)
                for j in range(TILES):
                    pool.indirect_dma_start(
                        yg[:, q % 2, j * F:(j + 1) * F], None, ytab,
                        bass.IndirectOffsetOnAxis(ap=idx[:, q, j:j + 1], axis=0)
                    ).then_inc(gathered[q % 2], 16)

            for q in range(U):
                gather(0, q)
            with pool.Fori(1, NI) as i:
                for q in range(U):
                    gather(i, q)

            def add_window(i, q):
                g = U * i + q
                base = nc.values_load(basei[0:1, bass.ds(g, 1)], engines=(mybir.EngineType.Pool,), min_val=0,
                                      max_val=N, skip_runtime_bounds_check_because="dst holds node numbers")
                pool.wait_ge(wsum_ready, g + 1)
                if not first(i, q, 1):
                    pool.wait_ge(agg_added, g)
                w = agg[:, bass.ds(base, WIN)]
                pool.tensor_tensor(w, w, wsum[:, q, :], ALU.add).then_inc(agg_added, 1)

            wide = pool.value_load(rowi[0:1, 0:1], min_val=0, max_val=N)
            pool.wait_ge(agg_set, 2)
            pool.tensor_scalar(agg[:, :], agg[:, :], c(C_U), -1.0, ALU.mult, ALU.mult).then_inc(agg_set, 1)
            pool.wait_ge(agg_set, 3)
            with pool.If(wide < WIN):
                for i in range(2):
                    for q in range(U):
                        add_window(i, q)
                with pool.Fori(1, NI // 2) as k:
                    for i in (2 * k, 2 * k + 1):
                        for q in range(U):
                            add_window(i, q)
                pool.wait_ge(agg_added, NG)
                pool.drain().then_inc(sums_over, 1)
            pool.wait_ge(sums_over, 1)
            pool.wait_ge(s_rcb, 16 * (RCN + 1))
            for c0, cw in CHUNKS[DVE_MEAN:]:
                pool.tensor_tensor(agg[:, c0:c0 + cw], agg[:, c0:c0 + cw], cnt[:, c0:c0 + cw], ALU.mult
                                   ).then_inc(s_meanp, 1)
            pool.wait_ge(s_nodein, NODEIN)
            pool.tensor_scalar(nbl[0:PN, :], blr[0:PN, :], -1.0, None, ALU.mult).then_inc(s_bl, 1)
            for t in range(NT):
                rows = xn[0:PN, t * F:(t + 1) * F]
                last = pool.tensor_tensor(rows, rows, blr[0:PN, :], ALU.add)
            last.then_inc(s_bl, 1)
            pool.wait_ge(s_bl, 2)
            for b in POOL_Z:
                t0, n = BATCH[b]
                zb = z[0:PN, t0 * F:(t0 + n) * F]
                pool.wait_ge(s_relu, b + 1)
                pool.tensor_tensor(zb, zb, xn[0:PN, t0 * F:(t0 + n) * F], ALU.add).then_inc(s_z, 1)

        @block.tensor
        def _(pe):
            pe.wait_ge(s_ident, 1)
            def turn_lists():
                pe.wait_ge(s_rowf, 2)
                for k, r in enumerate((srowf, drowf)):
                    rv = r[0:NG, :].rearrange("g (p j) -> g j p", j=TILES)
                    for j in range(TILES):
                        last = pe.transpose((psS, psX)[k][:, j * NG:(j + 1) * NG], rv[:, j, :], ident[0:NG, 0:NG])
                    last.then_inc(s_rowt, 1)
                pe.transpose(psT[0][0:1, 0:NG], rowst[0:NG, 0:1], ident[0:NG, 0:NG])
                pe.transpose(psT[1][0:1, 0:NG], rowst[0:NG, 2:3], ident[0:NG, 0:NG]).then_inc(s_rowt, 1)

            xv = xn0[0:PN, :].rearrange("p (t f) -> p t f", t=NT)
            xtv = xt0.rearrange("f (p t) -> f t p", t=NT)

            def turn_x(b):
                t0, n = BATCH[b]
                pe.wait_ge(s_x[next(k for k, part in enumerate(XLOADS) if BATCH[b] in part)], 16)
                if b >= 2:
                    pe.wait_ge(s_xt, b - 1)
                for t in range(n):
                    last = pe.transpose(psC[b % 2][:, t * PN:(t + 1) * PN], xv[:, t0 + t, :], ident[0:PN, 0:PN])
                last.then_inc(s_xps, 1)

            LISTS = len(BATCH) - 1
            turn_x(0)
            for b, (t0, n) in enumerate(BATCH):
                if b + 1 < len(BATCH):
                    turn_x(b + 1)
                pe.wait_ge(s_xt, b + 1)
                if b == 0:
                    pe.wait_ge(s_wsgn, 1)
                if b == LISTS:
                    turn_lists()
                if b >= 2:
                    pe.wait_ge(s_ysb, b - 1)
                for t in range(n):
                    last = pe.matmul(psH[b % 2][0:PN, t * F:(t + 1) * F], xtv[:, t0 + t, :], w1x[:, :],
                                     start=True, stop=True)
                last.then_inc(s_yps, 1)
            pe.wait_ge(s_idx, 1)
            pe.wait_ge(s_set, 1)
            pe.wait_ge(s_wsgn, 2)

            def product(i, q):
                g = U * i + q
                pe.wait_ge(ea_loaded[q % 2], 16 * (2 * i + q // 2 + 1) if not (isinstance(i, int) and g == NG - 1)
                           else 16 * (2 * i + q // 2 + 4))
                if not first(i, q, 2):
                    pe.wait_ge(eat_ready, g - 1)
                for b in range(2):
                    last = pe.transpose(psT[q % 2][:, b * P:(b + 1) * P], ear[:, q % 2, b * P:(b + 1) * P], ident[:, :])
                last.then_inc(ea_turned, 1)
                pe.wait_ge(eat_ready, g + 1)
                if not first(i, q, 2):
                    pe.wait_ge(h_ready, g - 1)
                for b in range(2):
                    last = pe.matmul(psH[q % 2][:, b * 2 * F:(b + 1) * 2 * F], eat[:, q % 2, b * P:(b + 1) * P],
                                     w1e[:, :, :].rearrange("p a f -> p (a f)"), start=True, stop=True)
                last.then_inc(prod_ready, 1)

            def counts(i, q):
                g = U * i + q
                pe.wait_ge(hotb_ready, g + 1)
                if not first(i, q, 2):
                    pe.wait_ge(cnt_added, g - 1)
                for j in range(TILES):
                    last = pe.matmul(psC[q % 2][:, 0:WIN], onesb[:, :], hotb[:, q, j * WIN:(j + 1) * WIN],
                                     start=(j == 0), stop=(j == TILES - 1))
                last.then_inc(cnt_ps, 1)

            def x_product(i):
                pe.wait_ge(cnt_added, U * i + U - 1)
                for h in range(H2):
                    last = pe.matmul(psC[0][:, h * PN:(h + 1) * PN], w2x[:, h * P:(h + 1) * P],
                                     xt0[:, bass.ds(i * PN, PN)], start=True, stop=True)
                last.then_inc(x_ps, 1)

            def edge_step(i):
                for q in range(U):
                    product(i, q)
                    if q == 0 and not (isinstance(i, int) and i == 0):
                        pe.wait_ge(x_out, i)
                    counts(i, q)
                if not (isinstance(i, int) and i == NI - 1):
                    x_product(i)

            edge_step(0)
            with pe.Fori(1, NI - 1) as i:
                edge_step(i)
            edge_step(NI - 1)
            for k in range(2):
                pe.wait_ge(s_folded, k + 1)
                last = pe.matmul(psT[0][:, k:k + 1], sq_fold(k), ones[:, :], start=True, stop=True)
            last.then_inc(s_folded, 1)
            pe.wait_ge(s_uin, 1)
            pe.matmul(psX[:, 0:F], work[:, 3, F:2 * F], work[:, 3, 0:F], start=True, stop=True).then_inc(s_ups, 1)
            wide = pe.value_load(rowi[0:1, 0:1], min_val=0, max_val=N)

            def window_sum(i, q):
                g = U * i + q
                pe.wait_ge(m_ready, g + 1)
                pe.wait_ge(hotf_ready, g + 1)
                if not first(i, q, 4):
                    pe.wait_ge(wsum_ready, g - 3)
                for j in range(TILES):
                    n = min(WIN + BEYOND, (TILES - j) * WIN)
                    last = pe.matmul(psA[q][:, 0:n], mx[:, q, j * F:(j + 1) * F], hotf[:, q, j * WIN:j * WIN + n],
                                     start=(j == 0), stop=(j == TILES - 1))
                last.then_inc(summed, 1)

            pe.wait_ge(cnt_added, NG)
            with pe.If(wide < WIN):
                for q in range(U):
                    window_sum(0, q)
                with pe.Fori(1, NI) as i:
                    for q in range(U):
                        window_sum(i, q)
            with pe.Else():
                pe.wait_ge(g_base, 1)
                pe.matmul(psT[0][:, 0:NG], work[0:1, 3, F:2 * F], work[0:1, 2, 0:NG], start=True,
                          stop=True).then_inc(g_base, 1)
                with pe.Fori(0, NG) as g:
                    with pe.Fori(0, NB) as b:
                        pe.wait_ge(g_m, g + 1)
                        pe.wait_ge(g_hot, NB * g + b + 1)
                        for j in range(TILES):
                            pe.matmul(psH[0][:, 0:WIDE], mx[:, 0, j * F:(j + 1) * F], ghot[:, j * WIDE:(j + 1) * WIDE],
                                      start=(j == 0), stop=(j == TILES - 1))
                        for j in range(TILES):
                            last = pe.matmul(psH[1][:, 0:WIDE], work[:, 3, F:2 * F],
                                             ghot[:, j * WIDE:(j + 1) * WIDE], start=(j == 0), stop=(j == TILES - 1))
                        last.then_inc(g_summed, 1)

            pe.wait_ge(s_w2s, 1)
            for h in range(H2):
                last = pe.matmul(psX[:, 2 * F + h:2 * F + h + 1], w2[:, h * P:(h + 1) * P], c(C_U), start=True,
                                 stop=True)
            last.then_inc(s_w2s, 1)
            prods = [(n, h) for n in range(NC) for h in range(H2)]
            for k, (n, h) in enumerate(prods):
                c0, cw = CHUNKS[n]
                if n < DVE_MEAN:
                    pe.wait_ge(s_mean, n + 1)
                else:
                    pe.wait_ge(s_meanp, n + 1 - DVE_MEAN)
                if k >= len(BANK):
                    pe.wait_ge(s_h2, k - len(BANK) + 1)
                pe.matmul(BANK[k % len(BANK)][:, 0:cw], w2[:, h * P:(h + 1) * P], agg[:, c0:c0 + cw], start=True,
                          stop=True).then_inc(s_h2ps, 1)
            pe.wait_ge(s_h2, len(prods))
            for b, (t0, n) in enumerate(BATCH):
                pe.wait_ge(s_h2r, b + 1 if b < DVE_RELU else H2 * (b + 1) - DVE_RELU)
                pe.wait_ge(s_h2rd, min(b + 1, DVE_RELU))
                if b >= 4:
                    pe.wait_ge(s_relu, b - 3)
                for t in range(n):
                    o = BANK[b % 4][0:PN, t * F:(t + 1) * F]
                    for h in range(H2):
                        n0 = h * N + (t0 + t) * PN
                        last = pe.matmul(o, h2r[:, n0:n0 + PN], wl[:, h * F:(h + 1) * F], start=(h == 0),
                                         stop=(h == H2 - 1))
                last.then_inc(s_ops, 1)

        @block.scalar
        def _(act):
            act.dma_start(w1x[:, :], W1[0:F, :]).then_inc(s_w1x, 16)
            act.dma_start(gbc, g1.partition_broadcast(P)).then_inc(s_w1x, 16)
            for b, (t, n) in enumerate(BATCH):
                act.wait_ge(s_yps, b + 1)
                act.activation(ysb[0:PN, t * F:(t + n) * F], psH[b % 2][0:PN, 0:n * F], ACT.Copy).then_inc(s_ysb, 1)

            def turned(i, q):
                g = U * i + q
                act.wait_ge(ea_turned, g + 1)
                if not first(i, q, 2):
                    act.wait_ge(prod_ready, g - 1)
                act.activation(eat[:, q % 2, :], psT[q % 2][:, 0:2 * P], ACT.Copy).then_inc(eat_ready, 1)

            def store(i, q):
                g = U * i + q
                act.wait_ge(h_ready, g + 1)
                if q == KEEP:
                    act.dma_start(spill[bass.ds(i, 1), :, :].rearrange("a p f -> (a p) f"), hs[:, q % 2, :]
                                  ).then_inc(spilled, 16)
                elif q == KEEP - 1:
                    act.wait_ge(hotb_ready, U * i + U)
                    act.dma_start(hot_dram[bass.ds(i, 1), :, :].rearrange("a p w -> (a p) w"),
                                  hotb[:, :, :].rearrange("p q w -> p (q w)")).then_inc(hot_saved, 16)
                if not first(i, q, 2):
                    act.wait_ge(sq_summed, g - 1)
                act.activation(sq[:, q % 2, :], hs[:, q % 2, :], ACT.Square).then_inc(sq_ready, 1)
                if q < KEEP:
                    act.activation(resg(i, q), hs[:, q % 2, :], ACT.Copy).then_inc(kept, 1)

            def x_product_out(i):
                act.wait_ge(x_ps, i + 1)
                if not (isinstance(i, int) and i == 0):
                    act.wait_ge(x_saved, 16 * i)
                act.activation(h2x, psC[0][:, 0:H2 * PN], ACT.Copy).then_inc(x_out, 1)
                act.wait_ge(x_out, i + 1)
                act.dma_start(h2x_dram[bass.ds(i, 1), :, :].rearrange("a p c -> (a p) c"), h2x).then_inc(x_saved, 16)

            def edge_step(i):
                for q in range(U):
                    if q < U - 1:
                        turned(i, q + 1)
                    elif not (isinstance(i, int) and i == NI - 1):
                        turned(i + 1, 0)
                    store(i, q)
                if not (isinstance(i, int) and i == NI - 1):
                    x_product_out(i)

            act.wait_ge(s_idx, 1)
            turned(0, 0)
            edge_step(0)
            act.wait_ge(s_tab, TAB)
            with act.Fori(1, NI - 1) as i:
                edge_step(i)
            edge_step(NI - 1)
            act.wait_ge(s_bn1, 4)
            act.activation(c(C_SD), c(C_V), ACT.Sqrt).then_inc(s_sqrt1, 1)
            wide = act.value_load(rowi[0:1, 0:1], min_val=0, max_val=N)

            def hot_rows(i, q, par, uses):
                g = U * i + q
                if q == 0:
                    act.wait_ge(hot_back[par], 16 * uses)
                if not first(i, q, 4):
                    act.wait_ge(summed, g - 3)
                act.activation(hotf[:, q, :], (hotb, hotb2)[par][:, q, :], ACT.Copy).then_inc(hotf_ready, 1)

            def window_out(i, q):
                g = U * i + q
                act.wait_ge(summed, g + 1)
                if not first(i, q, 4):
                    act.wait_ge(agg_added, g - 3)
                act.activation(wsum[:, q, :], psA[q][:, 0:WIN], ACT.Copy).then_inc(wsum_ready, 1)

            def spread_step(i, par, uses):
                for q in range(U):
                    hot_rows(i, q, par, uses)
                    if q >= 2:
                        window_out(i, q - 2)
                    elif not (isinstance(i, int) and i == 0):
                        window_out(i - 1, q + 2)

            act.wait_ge(prod_ready, NG)
            with act.If(wide < WIN):
                for par in range(2):
                    spread_step(par, par, 1)
                with act.Fori(1, NI // 2) as k:
                    for par in range(2):
                        spread_step(2 * k + par, par, k + 1)
                for q in (2, 3):
                    window_out(NI - 1, q)

            for n, (c0, cw) in enumerate(CHUNKS):
                act.wait_ge(s_h2, H2 * (n + 1))
                hc = h2[:, N + c0:N + c0 + cw]
                if n >= 2:
                    act.wait_ge(s_sm2, 2 * (n - 1))
                for k, func in enumerate((ACT.Identity, ACT.Square)):
                    j0 = (n % 2 * 2 + k) * CH
                    act.activation(junk[:, j0:j0 + cw], hc, func, accum_out=sm2[:, k * NC + n:k * NC + n + 1]
                                   ).then_inc(s_sm2, 1)
            act.wait_ge(s_bn2, 2)
            act.activation(colh[:, 8:10], colh[:, 6:8], ACT.Sqrt).then_inc(s_sqrt2, 1)
            act.wait_ge(s_bn2, 5)
            zv = z[0:PN, :].rearrange("p (t f) -> p t f", t=NT)
            zov = zo[0:PN, :].rearrange("p (t f) -> p t f", t=NT)
            m3 = mv3[0:PN, :].rearrange("p (t k) -> p t k", k=2)

            def relu(n):
                c0, cw = CHUNKS[n]
                for h in range(H2 if n >= DVE_RELU else 1):
                    act.activation(h2r[:, h * N + c0:h * N + c0 + cw], h2[:, h * N + c0:h * N + c0 + cw], ACT.Relu,
                                   bias=colh[:, 12 + h:13 + h], scale=colh[:, 10 + h:11 + h]).then_inc(s_h2r, 1)

            for n in range(NC):
                relu(n)
            for b, (t0, n) in enumerate(BATCH):
                act.wait_ge(s_rag, b + 1)
                act.activation(rs3[0:PN, t0:t0 + n], m3[:, t0:t0 + n, 1], ACT.Sqrt, bias=epsc[0:PN, :]
                               ).then_inc(s_sqrt3, 1)
                if b >= 1:
                    normalise(act, b - 1, zv, zov)
            normalise(act, len(BATCH) - 1, zv, zov)

        @block.vector
        def _(dve):
            chain = [0]

            def link(ins):
                chain[0] += 1
                ins.then_inc(s_dv, 1)
                dve.wait_ge(s_dv, chain[0])

            dve.memset(w1e[:, :, :], 0.0).then_inc(s_w, 1)
            dve.wait_ge(s_w1x, 32)
            link(dve.tensor_scalar(sgn, gbc, 0.0, 2.0, ALU.is_ge, ALU.mult))
            link(dve.tensor_scalar(sgn, sgn, -1.0, None, ALU.add))
            dve.tensor_tensor(w1x[:, :], w1x[:, :], sgn, ALU.mult).then_inc(s_wsgn, 1)
            xtv = xt0.rearrange("f (p t) -> f t p", t=NT)

            def turned_x(b):
                t0, n = BATCH[b]
                dve.wait_ge(s_xps, b + 1)
                dve.tensor_copy(xtv[:, t0:t0 + n, :], psC[b % 2][:, 0:n * PN].rearrange("f (t p) -> f t p", t=n)
                                ).then_inc(s_xt, 1)

            def stage_idx(i, q):
                dve.tensor_copy(idx[:, q, :].unsqueeze(2), srci[:, :, bass.ds(U * i + q, 1)]).then_inc(idx_staged, 1)

            turned_x(0)
            turned_x(1)
            dve.wait_ge(s_rows, 64)
            dve.tensor_copy(srowf[0:NG, :], srow[0:NG, :].bitcast(I32))
            link(dve.tensor_copy(drowf[0:NG, :], drow[0:NG, :].bitcast(I32)))
            turned_x(2)
            dve.tensor_reduce(rowst[0:NG, 0:1], drowf[0:NG, :], AX_X, ALU.min)
            turned_x(3)
            link(dve.tensor_reduce(rowst[0:NG, 1:2], drowf[0:NG, :], AX_X, ALU.max))
            turned_x(4)
            dve.tensor_scalar(drowf[0:NG, :], drowf[0:NG, :], rowst[0:NG, 0:1], None, ALU.subtract).then_inc(s_rowf, 1)
            dve.tensor_tensor(rowst[0:NG, 2:3], rowst[0:NG, 1:2], rowst[0:NG, 0:1], ALU.subtract).then_inc(s_rowf, 1)
            for b in range(5, len(BATCH)):
                turned_x(b)
            dve.wait_ge(s_rowt, 3)
            link(dve.tensor_copy(srci[:, :, :].rearrange("p j g -> p (j g)"), psS[:, 0:TILES * NG]))
            for q in range(U):
                stage_idx(0, q)
            dve.wait_ge(s_cols, 16 * 6)
            for a in range(2):
                last = dve.tensor_tensor(w1e[:, a, :], w1e[:, a, :], sgn, ALU.mult)
            last.then_inc(s_wsgn, 1)
            dve.tensor_copy(loc[:, :, :].rearrange("p j g -> p (j g)"), psX[:, 0:TILES * NG])
            link(dve.tensor_reduce(rowc[0:1, 0:1], psT[1][0:1, 0:NG], AX_X, ALU.max))
            dve.tensor_copy(rowi[0:1, 0:1], rowc[0:1, 0:1])
            link(dve.tensor_copy(basei[0:1, :], psT[0][0:1, 0:NG]))
            dve.memset(col[:, C_M:C_M + 1], 0.0).then_inc(s_idx, 1)

            def onehot_b(i, q):
                g = U * i + q
                if not first(i, q, 4):
                    dve.wait_ge(cnt_ps, g - 3)
                    dve.wait_ge(hot_saved, 16 * i)
                dve.tensor_tensor(hotb[:, q, :].rearrange("p (j w) -> p j w", j=TILES),
                                  iota[:, :].unsqueeze(1).broadcast_to([P, TILES, WIN]),
                                  loc[:, :, bass.ds(g, 1)].broadcast_to([P, TILES, WIN]), ALU.is_equal).then_inc(hotb_ready, 1)

            def add_counts(i, q):
                g = U * i + q
                base = dve.value_load(basei[0:1, bass.ds(g, 1)], min_val=0, max_val=N)
                dve.wait_ge(cnt_ps, g + 1)
                if not first(i, q, 1):
                    dve.wait_ge(cnt_added, g)
                w = cnt[:, bass.ds(base, WIN)]
                dve.tensor_tensor(w, w, psC[q % 2][:, 0:WIN], ALU.add).then_inc(cnt_added, 1)

            def make_h(i, q):
                g = U * i + q
                dve.wait_ge(prod_ready, g + 1)
                dve.wait_ge(gathered[q % 2], 64 * (2 * i + q // 2 + 1))
                if not first(i, q, 2):
                    dve.wait_ge(h_summed, g - 1)
                    dve.wait_ge(sq_ready, g - 1)
                    if q == 1:
                        dve.wait_ge(spilled, 16 * i)
                    else:
                        dve.wait_ge(kept, {0: 3 * i, 2: 3 * i + 1, 3: 3 * i + 2}[q])
                dve.tensor_tensor(hs[:, q % 2, :], psH[q % 2][:, :], yg[:, q % 2, :], ALU.add).then_inc(h_ready, 1)

            def sum_h(i, q):
                g = U * i + q
                dve.wait_ge(h_ready, g + 1)
                if not first(i, q, 1):
                    dve.wait_ge(h_summed, g)
                dve.tensor_tensor(psS[:, :], hs[:, q % 2, :], psS[:, :], ALU.add).then_inc(h_summed, 1)

            def sum_sq(i, q):
                g = U * i + q
                dve.wait_ge(sq_ready, g + 1)
                if not first(i, q, 1):
                    dve.wait_ge(sq_summed, g)
                dve.tensor_tensor(psX[:, :], sq[:, q % 2, :], psX[:, :], ALU.add).then_inc(sq_summed, 1)

            def fold(k, ps):
                dve.tensor_reduce(sq_fold(k), ps[:, :].rearrange("p (j f) -> p f j", j=TILES), AX_X, ALU.add
                                  ).then_inc(s_folded, 1)

            def edge_step(i):
                for q in range(U):
                    make_h(i, q)
                    if not (isinstance(i, int) and i == NI - 1):
                        stage_idx(i + 1, q)
                    if q < U - 1:
                        onehot_b(i, q + 1)
                    elif not (isinstance(i, int) and i == NI - 1):
                        onehot_b(i + 1, 0)
                    sum_h(i, q)
                    add_counts(i, q)
                    if isinstance(i, int) and U * i + q == NG - 1:
                        dve.wait_ge(h_summed, NG)
                        dve.wait_ge(sq_summed, NG - 1)
                        fold(0, psS)
                    sum_sq(i, q)

            dve.wait_ge(s_set, 1)
            dve.wait_ge(s_idx, 1)
            link(dve.tensor_scalar(c(C_AG), c(C_G), 0.0, 2.0, ALU.is_ge, ALU.mult))
            link(dve.tensor_scalar(c(C_AG), c(C_AG), -1.0, None, ALU.add))
            link(dve.tensor_tensor(c(C_B1), c(C_B1), c(C_AG), ALU.mult))
            link(dve.tensor_tensor(c(C_AG), c(C_G), c(C_AG), ALU.mult))
            link(dve.tensor_scalar(c(C_AG), c(C_AG), TINY, None, ALU.max))
            link(dve.reciprocal(c(C_T), c(C_AG)))
            link(dve.tensor_tensor(c(C_T), c(C_T), c(C_BE), ALU.mult))
            onehot_b(0, 0)
            dve.memset(psS[:, :], 0.0)
            dve.memset(psX[:, :], 0.0)
            edge_step(0)
            with dve.Fori(1, NI - 1) as i:
                edge_step(i)
            edge_step(NI - 1)

            def mark_edgeless(half):
                if half == 0:
                    dve.wait_ge(x_saved, 16 * NT)
                cut = slice(half * NAGG // 2, (half + 1) * NAGG // 2)
                dve.tensor_scalar(agg[:, cut], cnt[:, cut], 0.0, None, ALU.is_equal).then_inc(agg_set, 1)

            dve.wait_ge(cnt_added, NG)
            dve.wait_ge(sq_summed, NG)
            fold(1, psX)
            mark_edgeless(0)
            def bn(ins):
                bnc[0] += 1
                ins.then_inc(s_bn1, 1)
                dve.wait_ge(s_bn1, bnc[0])

            bnc = [0]
            dve.wait_ge(s_folded, 3)
            bn(dve.tensor_scalar(c(C_M, 2), psT[0][:, 0:2], 1.0 / E, None, ALU.mult))
            bn(dve.tensor_tensor(c(C_V), c(C_M), c(C_M), ALU.mult))
            bn(dve.tensor_tensor(c(C_V), c(C_Q), c(C_V), ALU.subtract))
            bn(dve.tensor_scalar(c(C_V), c(C_V), 0.0, EPS, ALU.max, ALU.add))
            bn(dve.tensor_tensor(c(C_M), c(C_M), c(C_B1), ALU.add))
            bn(dve.tensor_tensor(c(C_M), c(C_B1), c(C_M), ALU.subtract))
            dve.wait_ge(s_sqrt1, 1)
            bn(dve.scalar_tensor_tensor(out=c(C_U), in0=c(C_T), scalar=c(C_SD), in1=c(C_M), op0=ALU.mult,
                                        op1=ALU.add))
            dve.wait_ge(spilled, 16 * NI)
            dve.tensor_scalar(work[:, 3, 0:F], ident[:, :], c(C_U), -1.0, ALU.mult, ALU.mult)
            dve.memset(work[:, 3, F:2 * F], 1.0).then_inc(s_uin, 1)
            bn(dve.reciprocal(c(C_R), c(C_SD)))
            bn(dve.tensor_tensor(c(C_S), c(C_R), c(C_AG), ALU.mult))
            mark_edgeless(1)
            dve.wait_ge(s_ups, 1)

            def maxes(i, q):
                g = U * i + q
                if not first(i, q, 4):
                    dve.wait_ge(summed, g - 3)
                if q < KEEP:
                    hin = resg(i, q)
                else:
                    dve.wait_ge(reload, 16 * (i + 1))
                    hin = back if isinstance(i, int) and i == 0 else resg(i - 1, 0)
                dve.tensor_tensor(tiles(mx[:, q, :]), tiles(hin), negu, ALU.max).then_inc(m_ready, 1)

            def sum_step(i):
                for q in range(U):
                    maxes(i, q)

            dve.wait_ge(kept, NI * KEEP)
            wide = dve.value_load(rowi[0:1, 0:1], min_val=0, max_val=N)
            with dve.If(wide < WIN):
                sum_step(0)
                sum_step(1)
                invert_counts(dve)
                with dve.Fori(2, NI) as i:
                    sum_step(i)
            with dve.Else():
                general(dve, resg)
            dve.wait_ge(s_nodein, NODEIN)
            dve.tensor_scalar(w2, w2, c(C_S), None, ALU.mult).then_inc(s_w2s, 1)
            dve.wait_ge(sums_over, 1)
            dve.wait_ge(s_rcb, 16 * (RCN + 1))

            for c0, cw in CHUNKS[:DVE_MEAN]:
                dve.tensor_tensor(agg[:, c0:c0 + cw], agg[:, c0:c0 + cw], cnt[:, c0:c0 + cw], ALU.mult
                                  ).then_inc(s_mean, 1)
            bsv = bs2.rearrange("p (n s) -> p n s", s=6)
            for n, (c0, cw) in enumerate(CHUNKS):
                for h in range(H2):
                    k = H2 * n + h
                    dve.wait_ge(s_h2ps, k + 1)
                    hc = h2[:, h * N + c0:h * N + c0 + cw]
                    dve.tensor_tensor(hc, BANK[k % len(BANK)][:, 0:cw], hc, ALU.add).then_inc(s_h2, 1)
                dve.wait_ge(s_h2, H2 * n + 1)
                dve.bn_stats(bsv[:, n, :], h2[:, c0:c0 + cw]).then_inc(s_h2st, 1)
            dve.wait_ge(s_w2s, 2)
            dve.tensor_tensor(k2[:, 4:6], k2[:, 4:6], psX[:, 2 * F:2 * F + H2], ALU.add)
            dve.wait_ge(s_h2st, NC)
            dve.bn_aggr(mv2[:, 0:2], bs2)
            dve.wait_ge(s_sm2, 2 * NC)
            link(dve.tensor_reduce(mv2[:, 2:4], sm2.rearrange("p (k n) -> p k n", k=2), AX_X, ALU.add))
            link(dve.tensor_scalar(mv2[:, 2:4], mv2[:, 2:4], 1.0 / N, None, ALU.mult))
            link(dve.tensor_tensor(colh[:, 6:7], mv2[:, 2:3], mv2[:, 2:3], ALU.mult))
            bn2 = [0]

            def b2n(ins):
                bn2[0] += 1
                ins.then_inc(s_bn2, 1)
                dve.wait_ge(s_bn2, bn2[0])

            mvv = mv2.rearrange("p (h k) -> p h k", k=2)
            b2n(dve.tensor_tensor(mv2[:, 3:4], mv2[:, 3:4], colh[:, 6:7], ALU.subtract))
            b2n(dve.tensor_scalar(colh[:, 6:8], mvv[:, :, 1], 0.0, EPS, ALU.max, ALU.add))
            b2n(dve.tensor_tensor(colh[:, 14:16], mvv[:, :, 0], k2[:, 4:6], ALU.add))
            link(dve.tensor_tensor(colh[:, 14:16], k2[:, 4:6], colh[:, 14:16], ALU.subtract))
            dve.wait_ge(s_sqrt2, 1)
            link(dve.reciprocal(colh[:, 10:12], colh[:, 8:10]))
            b2n(dve.tensor_tensor(colh[:, 10:12], colh[:, 10:12], k2[:, 0:2], ALU.mult))
            for h in range(H2):
                last = dve.scalar_tensor_tensor(out=colh[:, 12 + h:13 + h], in0=colh[:, 14 + h:15 + h],
                                                scalar=colh[:, 10 + h:11 + h], in1=k2[:, 2 + h:3 + h], op0=ALU.mult,
                                                op1=ALU.add)
            b2n(last)
            dve.wait_ge(s_h2, NC * H2)
            for k in range(DVE_RELU + 1):
                for part, n in ((0, k), (1, k - 1)):
                    if not 0 <= n < DVE_RELU:
                        continue
                    c0, cw = CHUNKS[n]
                    hc = h2[:, N + c0:N + c0 + cw]
                    if part == 0:
                        dve.tensor_scalar(hc, hc, colh[:, 11:12], colh[:, 13:14], ALU.mult, ALU.add
                                          ).then_inc(s_h2n, 1)
                    else:
                        dve.wait_ge(s_h2n, n + 1)
                        dve.tensor_scalar(h2r[:, N + c0:N + c0 + cw], hc, 0.0, None, ALU.max).then_inc(s_h2rd, 1)
            zv = z[0:PN, :].rearrange("p (t f) -> p t f", t=NT)
            b3 = bs3[0:PN, :].rearrange("p (t s) -> p t s", s=6)
            m3 = mv3[0:PN, :].rearrange("p (t s) -> p t s", s=2)

            def out_max(b):
                t0, n = BATCH[b]
                dve.wait_ge(s_ops, b + 1)
                dve.tensor_tensor(zv[:, t0:t0 + n, :],
                                  BANK[b % 4][0:PN, 0:n * F].rearrange("p (t f) -> p t f", t=n),
                                  nbl[0:PN, :].unsqueeze(1).broadcast_to([PN, n, F]), ALU.max).then_inc(s_relu, 1)
                if b not in POOL_Z:
                    zb = z[0:PN, t0 * F:(t0 + n) * F]
                    dve.wait_ge(s_relu, b + 1)
                    dve.tensor_tensor(zb, zb, xn[0:PN, t0 * F:(t0 + n) * F], ALU.add).then_inc(s_zd, 1)

            def row_stats(b):
                t0, n = BATCH[b]
                if b in POOL_Z:
                    dve.wait_ge(s_z, POOL_Z.index(b) + 1)
                else:
                    dve.wait_ge(s_zd, b + 1 - sum(k < b for k in POOL_Z))
                for t in range(t0, t0 + n):
                    ins = dve.bn_stats(b3[:, t, :], zv[:, t, :])
                ins.then_inc(s_rst, 1)

            def join_stats(b):
                t0, n = BATCH[b]
                dve.wait_ge(s_rst, b + 1)
                for t in range(t0, t0 + n):
                    ins = dve.bn_aggr(m3[:, t, :], b3[:, t, :])
                ins.then_inc(s_rag, 1)

            def rstd(b):
                t0, n = BATCH[b]
                dve.wait_ge(s_sqrt3, b + 1)
                dve.reciprocal(rs3[0:PN, t0:t0 + n], rs3[0:PN, t0:t0 + n]).then_inc(s_rs, 1)

            def shift(b):
                t0, n = BATCH[b]
                dve.wait_ge(s_rs, b + 1)
                dve.scalar_tensor_tensor(out=nm3[0:PN, t0:t0 + n], in0=m3[:, t0:t0 + n, 0], scalar=-1.0,
                                         in1=rs3[0:PN, t0:t0 + n], op0=ALU.mult, op1=ALU.mult).then_inc(s_ln, 1)

            zov = zo[0:PN, :].rearrange("p (t f) -> p t f", t=NT)

            def norm_last(b):
                t = sum(BATCH[b]) - 1
                if DVE_NORM[b]:
                    dve.wait_ge(s_ln, b + 1)
                    dve.tensor_scalar(zov[:, t, :], zv[:, t, :], rs3[0:PN, t:t + 1], nm3[0:PN, t:t + 1], ALU.mult,
                                      ALU.add).then_inc(s_zod, 1)

            dve.wait_ge(s_bl, 2)
            NBT = len(BATCH)
            for b in range(NBT + 2):
                steps = [(out_max, b), (rstd, b - 2), (row_stats, b - 1), (shift, b - 2), (join_stats, b - 1),
                         (norm_last, b - 2)]
                if b == 1:
                    steps = [(row_stats, 0), (join_stats, 0), (out_max, 1)]
                for step, batch in steps:
                    if 0 <= batch < NBT:
                        step(batch)


_INS = ['x', 'src', 'dst', 'edge_attr_64', 'L0_gnn_W1', 'L0_gnn_b1', 'L0_gnn_g1', 'L0_gnn_be1', 'L0_gnn_W2',
        'L0_gnn_b2', 'L0_gnn_g2', 'L0_gnn_be2', 'L0_gnn_Wl', 'L0_gnn_bl']


def kernel(**inputs):
    import numpy as np
    import concourse.bacc as bacc
    from concourse.bass_utils import run_bass_kernel_spmd as run

    nc = bacc.Bacc("TRN2", target_bir_lowering=False, num_devices=1)
    arrays, args = {}, []
    for name in _INS:
        a = np.ascontiguousarray(inputs[name])
        arrays[f"in_{name}"] = a
        args.append(nc.dram_tensor(f"in_{name}", a.shape, mybir.dt.from_np(a.dtype), kind="ExternalInput").ap())
    shape = inputs['x'].shape
    args.append(nc.dram_tensor("out_dram", shape, F32, kind="ExternalOutput").ap())
    gnn_kernel(nc, *args)
    r = run(nc, [arrays], core_ids=[0])
    return r.results[0]["out_dram"]
```
